# Optimizing a Trainium2 kernel written in Bass

```python
import numpy as np
import jax
import jax.numpy as jnp

def _softmax(x, axis=-1):
    return jax.nn.softmax(x, axis=axis)

def _gelu(x):
    return jax.nn.gelu(x, approximate=True)

def _silu(x):
    return jax.nn.silu(x)

def _sigmoid(x):
    return jax.nn.sigmoid(x)

def _layernorm(x, axis=-1, eps=1e-05):
    m = jnp.mean(x, axis=axis, keepdims=True)
    v = jnp.var(x, axis=axis, keepdims=True)
    return (x - m) / jnp.sqrt(v + eps)

def _scatter_add(tgt, idx, src, axis=0):
    return tgt.at[idx].add(src)

def _segment_sum(src, seg, n):
    return jax.ops.segment_sum(src, seg, n)
kernel_name = 'mk_adaln_ffn_d1_seqx_r8_f92179'

def setup_inputs(seed: int=0):
    np.random.seed(seed)
    _w = jnp.asarray

    def _rec_inputs():
        import jax
        import jax.numpy as jnp
        _rk = jax.random.key(seed)
        x = 7.22e-05 + 1 * jax.random.normal(jax.random.fold_in(_rk, 1), (16, 128, 256), jnp.float32)
        _lenS = 128 - jax.random.randint(jax.random.fold_in(_rk, 7), (16,), 0, max(1, 128 // 4) + 1, jnp.int32)
        _lenS2 = 128 - jax.random.randint(jax.random.fold_in(_rk, 8), (16,), 0, max(1, 128 // 4) + 1, jnp.int32)
        cond_2048 = jax.random.bernoulli(jax.random.fold_in(_rk, 11), 0.5063, (16, 256)).astype(jnp.float32)
        return (x, cond_2048)
    x, cond_2048 = _rec_inputs()

    def _L0_cond_setup():
        import jax, jax.numpy as jnp
        import numpy as np
        NH = 8
        NEG = -1e+30
        key = jax.random.key(seed)
        k1, k2, k3, k4 = jax.random.split(key, 4)
        B, D, T = (4, 128, 256)
        x = jax.random.normal(k1, (B, D, T), dtype=jnp.float32)
        mask = jax.random.randint(k2, (B, T), 0, 2).astype(jnp.float32)
        lim = float(np.sqrt(6.0 / (D + D)))
        Wq = jax.random.uniform(k3, (D, D), dtype=jnp.float32, minval=-lim, maxval=lim)
        Wo = jax.random.uniform(k4, (D, D), dtype=jnp.float32, minval=-lim, maxval=lim)
        return {'x': x, 'mask': mask, 'Wq': Wq, 'Wo': Wo}
    _L0_cond_all = _L0_cond_setup()
    _L0_cond_in = {k: v for k, v in _L0_cond_all.items() if k in ('Wq', 'Wo')}
    del _L0_cond_all

    def _L0_ffn_setup():
        import jax, jax.numpy as jnp
        import numpy as np
        B, S, H, I, E = (2, 256, 256, 176, 8)
        TOP_K = 2
        key = jax.random.key(seed)
        k0, k1, k2, k3, k4 = jax.random.split(key, 5)
        scale = float(np.sqrt(2.0 / (H + I)))
        return {'hidden_states': jax.random.normal(k0, (B, S, H), dtype=jnp.float32), 'router_w': jax.random.normal(k1, (E, H), dtype=jnp.float32) * H ** (-0.5), 'gate_w': jax.random.normal(k2, (E, I, H), dtype=jnp.float32) * scale, 'up_w': jax.random.normal(k3, (E, I, H), dtype=jnp.float32) * scale, 'down_w': jax.random.normal(k4, (E, H, I), dtype=jnp.float32) * scale}
    _L0_ffn_all = _L0_ffn_setup()
    _L0_ffn_in = {k: v for k, v in _L0_ffn_all.items() if k in ('router_w', 'gate_w', 'up_w', 'down_w')}
    del _L0_ffn_all
    return {'x': x, 'cond_2048': cond_2048, 'L0_cond_Wq': _L0_cond_in['Wq'], 'L0_cond_Wo': _L0_cond_in['Wo'], 'L0_ffn_router_w': _L0_ffn_in['router_w'], 'L0_ffn_gate_w': _L0_ffn_in['gate_w'], 'L0_ffn_up_w': _L0_ffn_in['up_w'], 'L0_ffn_down_w': _L0_ffn_in['down_w']}

def reference(x, cond_2048, L0_cond_Wq, L0_cond_Wo, L0_ffn_router_w, L0_ffn_gate_w, L0_ffn_up_w, L0_ffn_down_w):
    import jax
    import jax.numpy as jnp

    def _L0_cond_ref(x, mask, Wq, Wo):
        import jax, jax.numpy as jnp
        import numpy as np
        NH = 8
        NEG = -1e+30
        B, D, T = x.shape
        dk = D // NH
        scale = 1.0 / jnp.sqrt(jnp.asarray(dk, x.dtype))
        xt = jnp.transpose(x, (0, 2, 1))
        q = xt @ Wq.T
        qh = q.reshape(B, T, NH, dk).transpose(0, 2, 1, 3)
        scores = scale * jnp.einsum('bhqd,bhkd->bhqk', qh, qh)
        cmask = mask[:, None, None, :]
        rmask = mask[:, None, :, None]
        logits = (scores * cmask + (1.0 - cmask) * NEG) * rmask
        attn = jax.nn.softmax(logits, axis=-1)
        ctx = jnp.einsum('bhqk,bhkd->bhqd', attn, qh)
        ctx = ctx.transpose(0, 2, 1, 3).reshape(B, T, D)
        out = ctx @ Wo.T
        return jnp.transpose(out, (0, 2, 1))

    def _L0_ffn_ref(hidden_states, router_w, gate_w, up_w, down_w):
        import jax, jax.numpy as jnp
        import numpy as np
        B, S, H, I, E = (2, 256, 256, 176, 8)
        TOP_K = 2
        b, s, h = hidden_states.shape
        e = router_w.shape[0]
        x = hidden_states.reshape(-1, h)
        logits = jnp.einsum('th,eh->te', x, router_w)
        top_vals, top_idx = jax.lax.top_k(logits, TOP_K)
        top_w = jax.nn.softmax(top_vals, axis=-1)
        expert = top_idx[:, 0]
        weight = top_w[:, 0]
        gate = jnp.einsum('th,eih->eti', x, gate_w)
        up = jnp.einsum('th,eih->eti', x, up_w)
        act = jax.nn.silu(gate) * up
        out_e = jnp.einsum('eti,ehi->eth', act, down_w)
        combine = jax.nn.one_hot(expert, e, dtype=x.dtype) * weight[:, None]
        out = jnp.einsum('eth,te->th', out_e, combine)
        return out.reshape(b, s, h)
    x = x + _L0_ffn_ref(_L0_cond_ref(x, cond_2048, L0_cond_Wq, L0_cond_Wo), L0_ffn_router_w, L0_ffn_gate_w, L0_ffn_up_w, L0_ffn_down_w)
    return x

_drawn_inputs = setup_inputs


def setup_inputs(seed=0):
    import zlib

    import numpy as np

    out = dict(_drawn_inputs(seed))
    spreads = {}
    factors = {}
    for name, (base, spread) in spreads.items():
        noise = np.random.default_rng([zlib.crc32(name.encode()), seed]).standard_normal(out[name].shape)
        drawn = base * np.exp(spread * noise) if base else spread * noise
        out[name] = jnp.asarray(drawn.astype(out[name].dtype))
    for name, factor in factors.items():
        out[name] = (out[name] * factor).astype(out[name].dtype)
    return out
```

```python
from contextlib import ExitStack

import concourse.bass as bass
from concourse import mybir

F32 = mybir.dt.float32
BF16 = mybir.dt.bfloat16
I32 = mybir.dt.int32
U32 = mybir.dt.uint32
ALU = mybir.AluOpType
ACT = mybir.ActivationFunctionType
AX = mybir.AxisListType

P = 128
NEG = -1e30
NH = 8
DK = P // NH
RING = 3
SRING = 6
LEFT = [0, 1, 2, 0, 1, 0]
RIGHT = [0, 0, 0, 1, 1, 2]
LEFT_RUNS = [(0, 0, 3), (3, 0, 2), (5, 0, 1)]
RIGHT_RUNS = [(0, 0, 1), (1, 0, 1), (2, 0, 2), (4, 1, 2)]
ROW_MASK = len(LEFT) * DK
ROW_MAX = ROW_MASK + 1
ROWS1 = ROW_MASK + 1
ROWS2 = ROW_MAX + 2
STACK_DMAS = len(LEFT_RUNS) + len(RIGHT_RUNS) + 1


def adaln_ffn(nc, x, cond, wqT, woT, routerT, guT, dnT, out):
    B, D, T = x.shape
    E = routerT.shape[1]
    I2 = guT.shape[2]
    I = I2 // 2
    IR = I - P
    NT = T // P
    V1 = DK + 1
    TOK = B * D
    SLOT_TILES = TOK // P + E - 1
    NS = SLOT_TILES
    assert D == P and NT == 2 and B == 16

    ctx = ExitStack()
    with ctx:
        def sb(name, shape, dt=F32):
            return ctx.enter_context(nc.sbuf_tensor(name, shape, dt))

        def sem(name):
            return ctx.enter_context(nc.semaphore(name))

        def sems(name, n):
            return [sem(f"{name}{i}") for i in range(n)]

        bank = [ctx.enter_context(nc.psum_tensor(f"bank{i}", [P, 512], F32)) for i in range(8)]

        parts_dram = [nc.dram_tensor(f"parts_dram{r}", [2, 3, DK, NH, T], BF16, kind="Internal").ap() for r in range(RING)]
        mask_dram = nc.dram_tensor("mask_dram", [B, 2, NH, T], BF16, kind="Internal").ap()
        rows_dram = nc.dram_tensor("rows_dram", [TOK, 2 * T], F32, kind="Internal").ap()

        ident = sb("ident", [P, P])
        ident_b = sb("ident_b", [P, P], BF16)
        before = sb("before", [P, P], BF16)
        ones_b = sb("ones_b", [P, P], BF16)
        iota_p = sb("iota_p", [P, 1])
        iota_col = sb("iota_col", [P, P])
        iota_col_b = sb("iota_col_b", [P, P], BF16)
        iota_e = sb("iota_e", [P, B, E])
        iota_b = sb("iota_b", [P, B, NS], BF16)
        iota_s = sb("iota_s", [P, B, NS])
        fill = sb("fill", [P, E, B])
        tile_e = sb("tile_e", [1, NS, E])

        wq_sb = sb("wq_sb", [P, P])
        wo_sb = sb("wo_sb", [P, P])
        rt_sb = sb("rt_sb", [P, NT, E])
        gu_sb = sb("gu_sb", [P, NT, E, I2])
        dn_sb = sb("dn_sb", [P, E, T])
        dn2_sb = sb("dn2_sb", [IR, E, T])

        cond_sb = sb("cond_sb", [B, T])
        mask2 = sb("mask2", [B, 2, T], BF16)
        cond_all = sb("cond_all", [P, B, T])
        x_sb = sb("x_sb", [P, B, T])
        q_sb = sb("q_sb", [P, RING, T])
        rest = sb("rest", [P, T])
        parts = sb("parts", [P, RING, 2, 3, T], BF16)
        stack = [sb(f"stack{r}", [P, 2, NH, T], BF16) for r in range(RING)]
        v_sb = sb("v_sb", [P, RING, NT, NH, V1])
        row_max = sb("row_max", [P, 2, NT, NH // 2])
        neg_max = sb("neg_max", [P, 2, NT, 2, NH // 2], BF16)
        neg_rows = sb("neg_rows", [NH, 2, T], BF16)
        probs = sb("probs", [P, 2, NT, T])
        rsum = sb("rsum", [P, NT, NH])
        ctx_sb = sb("ctx_sb", [P, NT, P])
        ctxT = sb("ctxT", [P, T])
        h_sb = sb("h_sb", [P, RING, T])
        hT = sb("hT", [P, NT, P])
        logits = sb("logits", [P, B, E])

        top = sb("top", [P, B, E])
        gap = sb("gap", [P, B])
        gate = sb("gate", [P, B])
        picked = sb("picked", [P, B, E])
        first = sb("first", [P, B])
        onehot = sb("onehot", [P, B, E])
        onehot_b = sb("onehot_b", [P, B, E], BF16)
        count = sb("count", [P, E])
        filled = sb("filled", [P, E, B])
        tiles = sb("tiles", [P, E])
        tiles_to = sb("tiles_to", [P, E])
        one_e = sb("one_e", [P, E])
        idle = sb("idle", [1, 128])
        start = sb("start", [P, E])
        place = sb("place", [P, B, E])
        pos = sb("pos", [P, B])
        pos_i = sb("pos_i", [P, B], I32)
        hi_i = sb("hi_i", [P, B], I32)
        lo_i = sb("lo_i", [P, B], I32)
        hi = sb("hi", [P, B])
        lo = sb("lo", [P, B])
        lo_hot = sb("lo_hot", [P, B, P], BF16)
        cols = sb("cols", [P, B, 6, NS], BF16)
        w_part = sb("w_part", [P, 3, B], BF16)
        w_rest = sb("w_rest", [P, B])
        table = sb("table", [P, 6, NS])
        token = sb("token", [P, NS])
        token_f = sb("token_f", [P, NS])
        take_i = sb("take_i", [P, NS], I32)
        put_i = sb("put_i", [P, NS], I32)
        weight = sb("weight", [P, NS])
        expert_cmp = sb("expert_cmp", [1, NS, E])
        expert_f = sb("expert_f", [1, NS])
        expert_i = sb("expert_i", [1, NS], I32)

        take = [sb(f"take{r}", [P, 1], I32) for r in range(SRING)]
        put = [sb(f"put{r}", [P, 1], I32) for r in range(SRING)]
        got = [sb(f"got{r}", [P, 2 * T]) for r in range(SRING)]
        gotT = sb("gotT", [P, 2, NT, P])
        silu = sb("silu", [P, 2, I])
        act_sb = sb("act_sb", [P, 2, I])
        actT = sb("actT", [P, 2, NT, P])
        y_sb = [sb(f"y_sb{r}", [P, T]) for r in range(SRING)]

        consts_made = sem("consts_made")
        iotas_made = sem("iotas_made")
        cond_in = sem("cond_in")
        cond_all_in = sem("cond_all_in")
        weights_in = sem("weights_in")
        router_in = sem("router_in")
        experts_in = sem("experts_in")
        x_first_in = sem("x_first_in")
        x_rest_in = sem("x_rest_in")
        bias_made = sem("bias_made")
        mask_out = sem("mask_out")
        x_out = sem("x_out")
        q_done = sem("q_done")
        q_copied = sem("q_copied")
        parts_step = sem("parts_step")
        parts_made = sem("parts_made")
        parts_out = sems("parts_out", RING)
        stack_in = sems("stack_in", RING)
        vt_done = sem("vt_done")
        vt_copied = sem("vt_copied")
        s1_done = sem("s1_done")
        max_done = sem("max_done")
        neg_hi_made = sem("neg_hi_made")
        neg_made = sem("neg_made")
        neg_turned = sem("neg_turned")
        neg_copied = sem("neg_copied")
        max_in = sems("max_in", 2)
        s2_done = sem("s2_done")
        exp_done = sem("exp_done")
        pv_done = sem("pv_done")
        recip_done = sem("recip_done")
        norm_done = sem("norm_done")
        ctxT_done = sem("ctxT_done")
        ctxT_copied = sem("ctxT_copied")
        h_done = sem("h_done")
        h_copied = sem("h_copied")
        h_out = sems("h_out", RING)
        hT_done = sem("hT_done")
        hT_copied = sem("hT_copied")
        lg_done = sem("lg_done")
        lg_copied = sem("lg_copied")
        route_step = sem("route_step")
        gap_made = sem("gap_made")
        gap_exp = sem("gap_exp")
        onehot_made = sem("onehot_made")
        ranks_done = sem("ranks_done")
        cols_made = sem("cols_made")
        table_done = sem("table_done")
        take_made = sem("take_made")
        routed = sem("routed")
        took = sem("took")
        put_made = sem("put_made")
        got_in = sems("got_in", SRING)
        g_turned = sem("g_turned")
        g_copied = sem("g_copied")
        gu_done = sem("gu_done")
        silu_done = sem("silu_done")
        act_done = sem("act_done")
        a_turned = sem("a_turned")
        a_copied = sem("a_copied")
        dn_done = sem("dn_done")
        y_done = sem("y_done")
        y_out = sems("y_out", SRING)

        class Step:

            def __init__(self, c, j, n, items, peeled):
                self.c, self.j, self.n, self.items, self.peeled = c, j, n, items, peeled

            def has(self, d):
                return not self.peeled or 0 <= self.c + d < self.items

            def first(self, d, k):
                return self.peeled and self.c + d < k

            def at(self, d, times=1, plus=0):
                if self.peeled:
                    return times * (self.c + d) + plus
                return self.j * (self.n * times) + (times * (self.c + d) + plus)

            def slot(self, d):
                return (self.c + d) % self.n

            def use(self, d, times=1, plus=0):
                k = times * ((self.c + d) // self.n) + plus
                return k if self.peeled else self.j * times + k

        def run_steps(eng, step, n, items, first, loops, last):
            for c in range(first):
                step(Step(c, 0, n, items, True))
            with eng.Fori(0, loops) as j:
                for u in range(n):
                    step(Step(first + u, j, n, items, False))
            for c in range(first + n * loops, last):
                step(Step(c, 0, n, items, True))

        def attention_steps(eng, step):
            run_steps(eng, step, RING, B, 2, 4, B + 2)

        def expert_steps(eng, step):
            run_steps(eng, step, SRING, NS, 4, 3, NS + 3)

        block = ctx.enter_context(nc.Block())

        @block.gpsimd
        def _(pool):
            g = nc.gpsimd

            n_waits = [0]

            def wait_step(semaphore, value):
                pool.wait_ge(semaphore, value)
                if not isinstance(value, int):
                    n_waits[0] += 1
                    g.tensor_tensor(idle[:, n_waits[0]:n_waits[0] + 1], one_e[0:1, 0:1], one_e[0:1, 0:1], ALU.add)

            g.memset(ident[:, :], 0.0).then_inc(consts_made, 1)
            g.memset(before[:, :], 1.0).then_inc(consts_made, 1)
            g.memset(ones_b[:, :], 1.0).then_inc(consts_made, 1)
            pool.wait_ge(consts_made, 3)
            g.affine_select(out=ident[:, :], in_=ident[:, :], compare_op=ALU.not_equal, fill=1.0, base=0,
                            pattern=[[-1, P]], channel_multiplier=1).then_inc(consts_made, 1)
            g.affine_select(out=before[:, :], in_=before[:, :], compare_op=ALU.is_gt, fill=0.0, base=0,
                            pattern=[[1, P]], channel_multiplier=-1).then_inc(consts_made, 1)
            pool.wait_ge(consts_made, 5)
            g.tensor_copy(ident_b[:, :], ident[:, :]).then_inc(consts_made, 1)
            pool.wait_ge(consts_made, 6)
            for k in range(RING):
                g.memset(stack[k][ROW_MASK:P, :, :, :], 1.0).then_inc(consts_made, 1)
            pool.wait_ge(consts_made, 6 + RING)
            g.memset(v_sb[:, :, :, :, :], 1.0).then_inc(consts_made, 1)
            g.memset(one_e[:, :], 1.0).then_inc(consts_made, 1)
            pool.wait_ge(consts_made, 11)
            pool.wait_ge(cond_all_in, 16)

            def make_parts(st, d):
                k, pt = st.slot(d), parts[:, st.slot(d)]
                wait_step(q_copied, st.at(d, 1, 1))
                if not st.first(d, RING):
                    wait_step(parts_out[k], st.use(d, 96))
                g.tensor_copy(pt[:, 0, 0, :], q_sb[:, k, :]).then_inc(parts_step, 1)
                wait_step(parts_step, st.at(d, 3, 1))
                g.tensor_tensor(rest[:, :], q_sb[:, k, :], pt[:, 0, 0, :], ALU.subtract).then_inc(parts_step, 1)
                wait_step(parts_step, st.at(d, 3, 2))
                g.tensor_copy(pt[:, 0, 1, :], rest[:, :]).then_inc(parts_step, 1)
                wait_step(parts_step, st.at(d, 3, 3))
                g.tensor_tensor(pt[:, 0, 2, :], rest[:, :], pt[:, 0, 1, :], ALU.subtract).then_inc(parts_made, 1)
                wait_step(parts_made, st.at(d, 4, 1))
                b = st.at(d)
                mask = cond_all[:, bass.ds(b, 1), :].rearrange("p o t -> p (o t)")
                for p in range(3):
                    g.tensor_tensor(pt[:, 1, p, :], pt[:, 0, p, :], mask, ALU.mult).then_inc(parts_made, 1)

            make_parts(Step(0, 0, RING, B, True), 0)
            make_parts(Step(1, 0, RING, B, True), 0)

            def step(st):
                if st.has(2):
                    make_parts(st, 2)

            attention_steps(pool, step)

            def iota(ap, pattern, base=0, per_partition=0):
                g.iota(ap, pattern, base=base, channel_multiplier=per_partition,
                       allow_small_or_imprecise_dtypes=True).then_inc(iotas_made, 1)

            iota(iota_p[:, :], [[0, 1]], 0, 1)
            iota(iota_col_b[:, :], [[1, P]])
            iota(iota_e[:, :, :], [[0, B], [1, E]], -E)
            iota(iota_b[:, :, :], [[1, B], [0, NS]])
            iota(iota_s[:, :, :], [[0, B], [1, NS]])
            iota(fill[:, :, :], [[0, E], [P, B]])
            iota(tile_e[:, :, :], [[1, NS], [0, E]])

            for k in range(RING):
                pool.wait_ge(h_out[k], 16 * len(range(k, B, RING)))
            pool.wait_ge(x_out, 16)
            pool.wait_ge(take_made, 1)
            out_rows = out.rearrange("b d t -> (b d) t")

            def slot_step(st):
                c = st.slot(0)
                if st.has(-SRING):
                    wait_step(y_done, st.at(-SRING, 1, 1))
                    if not st.first(-SRING, SRING):
                        wait_step(y_out[c], st.use(-SRING, 16))
                    m = st.at(-SRING)
                    g.tensor_copy(put[c][:, :], put_i[:, bass.ds(m, 1)]).then_inc(put_made, 1)
                    wait_step(put_made, st.at(-SRING, 1, 1))
                    g.indirect_dma_start(out_rows, bass.IndirectOffsetOnAxis(ap=put[c][:, 0:1], axis=0),
                                         y_sb[c][:, :], None, bounds_check=TOK - 1,
                                         oob_is_err=False).then_inc(y_out[c], 16)
                if st.has(0):
                    if not st.first(0, SRING):
                        wait_step(got_in[c], st.use(0, 16))
                    n = st.at(0)
                    g.tensor_copy(take[c][:, :], take_i[:, bass.ds(n, 1)]).then_inc(took, 1)
                    wait_step(took, st.at(0, 1, 1))
                    g.indirect_dma_start(got[c][:, :], None, rows_dram[:, :],
                                         bass.IndirectOffsetOnAxis(ap=take[c][:, 0:1], axis=0)).then_inc(got_in[c], 16)

            run_steps(pool, slot_step, SRING, NS, SRING, 2, NS + SRING)
            for c in range(SRING):
                pool.wait_ge(y_out[c], 16 * len(range(c, NS, SRING)))

        @block.sync
        def _(sp):
            sp.dma_start(wq_sb[:, :], wqT).then_inc(weights_in, 16)
            sp.dma_start(x_sb[:, 0:2, :], x[0:2].rearrange("b d t -> d b t")).then_inc(x_first_in, 16)
            sp.dma_start(x_sb[:, 2:B, :], x[2:B].rearrange("b d t -> d b t")).then_inc(x_rest_in, 16)
            sp.dma_start(cond_sb[:, :], cond).then_inc(cond_in, 16)
            sp.dma_start(cond_all[:, :, :].rearrange("p b t -> p (b t)"),
                         cond.rearrange("(o b) t -> o (b t)", o=1).to_broadcast([P, B * T])).then_inc(cond_all_in, 16)
            sp.dma_start(wo_sb[:, :], woT).then_inc(weights_in, 16)
            sp.dma_start(rt_sb[:, :, :], routerT.rearrange("(k p) e -> p k e", p=P)).then_inc(router_in, 16)
            sp.wait_ge(bias_made, 2)
            for h in range(NH):
                sp.dma_start(mask_dram[:, :, h, :], mask2[:, :, :]).then_inc(mask_out, 16)

            def ready(st, *values):
                return values if st.peeled else [sp.snap(a) for a in values]

            def write_parts(st, d):
                k = st.slot(d)
                sp.wait_ge(parts_made, st.at(d, 4, 4))
                for side in range(2):
                    for p in range(3):
                        sp.dma_start(parts_dram[k][side, p].rearrange("k h t -> h k t"),
                                     parts[:, k, side, p, :]).then_inc(parts_out[k], 16)

            def read_stack(st, d):
                k = st.slot(d)
                b, = ready(st, st.at(d))
                if not st.first(d, RING):
                    sp.wait_ge(s2_done, st.at(d - RING, NH, NH))
                sp.dma_start(stack[k][ROW_MASK:ROW_MASK + 1, :, :, :],
                             mask_dram[bass.ds(b, 1), :, :, :]).then_inc(stack_in[k], 16)
                sp.wait_ge(parts_out[k], st.use(d, 96, 96))
                for side, runs in enumerate((LEFT_RUNS, RIGHT_RUNS)):
                    for row, p, n in runs:
                        sp.dma_start(stack[k][row * DK:(row + n) * DK, side, :, :],
                                     parts_dram[k][side, p:p + n].rearrange("p k h t -> (p k) h t")).then_inc(stack_in[k], 16)

            def write_max(st, d, half):
                sp.wait_ge(neg_copied, st.at(d, 2, half + 1))
                for p in range(2):
                    n = NH // 2
                    sp.dma_start(stack[st.slot(d)][ROW_MAX + p:ROW_MAX + p + 1, 1, half * n:half * n + n, :],
                                 neg_rows[p * n:p * n + n, half, :]).then_inc(max_in[half], 16)

            write_parts(Step(0, 0, RING, B, True), 0)
            sp.wait_ge(mask_out, 16 * NH)
            read_stack(Step(0, 0, RING, B, True), 0)
            write_parts(Step(1, 0, RING, B, True), 0)
            for k in range(NT):
                sp.dma_start(gu_sb[:, k, :, :], guT[:, k * P:(k + 1) * P, :].rearrange("e p i -> p e i")).then_inc(experts_in, 16)
            sp.dma_start(dn_sb[:, :, :], dnT[:, 0:P, :].rearrange("e i t -> i e t")).then_inc(experts_in, 16)
            sp.dma_start(dn2_sb[:, :, :], dnT[:, P:I, :].rearrange("e i t -> i e t")).then_inc(experts_in, 16)
            sp.dma_start(rows_dram[:, T:2 * T], x.rearrange("b d t -> (b d) t")).then_inc(x_out, 16)

            def step(st):
                if st.has(1):
                    read_stack(st, 1)
                if st.has(-1):
                    write_max(st, -1, 1)
                if st.has(2):
                    write_parts(st, 2)
                if st.has(-2):
                    t, copied = ready(st, st.at(-2, P), st.at(-2, 1, 1))
                    sp.wait_ge(h_copied, copied)
                    sp.dma_start(rows_dram[bass.ds(t, P), 0:T], h_sb[:, st.slot(-2), :]).then_inc(h_out[st.slot(-2)], 16)
                if st.has(0):
                    write_max(st, 0, 0)

            attention_steps(sp, step)

        @block.tensor
        def _(pe):
            t_ = nc.tensor

            def project_q(st, d):
                if st.first(d, 3):
                    pe.wait_ge(x_first_in if st.first(d, 2) else x_rest_in, 16)
                b = st.at(d)
                if not st.first(d, 1):
                    pe.wait_ge(q_copied, st.at(d))
                t_.matmul(bank[5][:, 0:T], wq_sb[:, :], x_sb[:, bass.ds(b, 1), :].rearrange("p o t -> p (o t)"), start=True, stop=True).then_inc(q_done, 1)

            def turn_values(st, d):
                pe.wait_ge(q_copied, st.at(d, 1, 1))
                if not st.first(d, 2):
                    pe.wait_ge(neg_copied, st.at(d - 2, 2, 2))
                elif not st.first(d, 1):
                    pe.wait_ge(vt_copied, 1)
                for k in range(NT):
                    mm = t_.transpose(bank[6][:, k * P:(k + 1) * P], q_sb[:, st.slot(d), k * P:(k + 1) * P], ident[:, :])
                mm.then_inc(vt_done, 1)

            def turn_max(st, d, half):
                pe.wait_ge(neg_made, st.at(d, 2, half + 1))
                last = d + (2 if half == 1 else 1)
                last = min(st.c + last, B) if st.peeled else st.at(last)
                pe.wait_ge(vt_copied, last if half == 1 else (min(st.c + d + 2, B) if st.peeled else st.at(d, 1, 2)))
                if half == 0 and not st.first(d, 1):
                    pe.wait_ge(neg_copied, st.at(d, 2))
                to = bank[6][:, :].bitcast(BF16)
                for q in range(NT):
                    mm = t_.transpose(to[0:NH, q * P:(q + 1) * P],
                                      neg_max[:, half, q, :, :].rearrange("p a h -> p (a h)"), ident_b[:, :])
                mm.then_inc(neg_turned, 1)

            def scores_for_max(st, h):
                k = st.slot(0)
                if h == 0:
                    pe.wait_ge(stack_in[k], st.use(0, 16 * STACK_DMAS, 16 * STACK_DMAS))
                if h >= 2 or not st.first(0, 1):
                    pe.wait_ge(max_done, st.at(0, NH, h - 1))
                for q in range(NT):
                    mm = t_.matmul(bank[h % 2][:, q * T:(q + 1) * T], stack[k][0:ROWS1, 1, h, q * P:(q + 1) * P],
                                   stack[k][0:ROWS1, 0, h, :], start=True, stop=True)
                mm.then_inc(s1_done, 1)

            def scores_for_exp(st, h):
                k = st.slot(-1)
                if h % 4 == 0:
                    pe.wait_ge(max_in[h // 4], st.at(-1, 32, 32))
                if h >= 2 or not st.first(-1, 1):
                    pe.wait_ge(exp_done, st.at(-1, NH, h - 1))
                for q in range(NT):
                    mm = t_.matmul(bank[2 + h % 2][:, q * T:(q + 1) * T], stack[k][0:ROWS2, 0, h, q * P:(q + 1) * P],
                                   stack[k][0:ROWS2, 1, h, :], start=True, stop=True)
                mm.then_inc(s2_done, 1)

            def apply_probs(st, h):
                pe.wait_ge(exp_done, st.at(-1, NH, h + 1))
                if h == 0:
                    if not st.first(-1, 1):
                        pe.wait_ge(norm_done, st.at(-1))
                    pe.wait_ge(vt_copied, st.at(-1, 1, 1))
                for q in range(NT):
                    for k in range(NT):
                        o = (q * NH + h) * V1
                        mm = t_.matmul(bank[4][:, o:o + V1], probs[:, h % 2, k, q * P:(q + 1) * P],
                                       v_sb[:, st.slot(-1), k, h, :], start=(k == 0), stop=(k == NT - 1))
                mm.then_inc(pv_done, 1)

            def turn_context(st):
                pe.wait_ge(norm_done, st.at(-2, 1, 1))
                if not st.first(-2, 1):
                    pe.wait_ge(lg_copied, st.at(-2))
                for k in range(NT):
                    mm = t_.transpose(bank[7][:, k * P:(k + 1) * P], ctx_sb[:, k, :], ident[:, :])
                mm.then_inc(ctxT_done, 1)

            def project_out(st):
                pe.wait_ge(ctxT_copied, st.at(-2, 1, 1))
                t_.matmul(bank[7][:, 0:T], wo_sb[:, :], ctxT[:, :], start=True, stop=True).then_inc(h_done, 1)

            def turn_hidden(st):
                pe.wait_ge(h_copied, st.at(-2, 1, 1))
                for k in range(NT):
                    mm = t_.transpose(bank[7][:, k * P:(k + 1) * P], h_sb[:, st.slot(-2), k * P:(k + 1) * P], ident[:, :])
                mm.then_inc(hT_done, 1)

            def router(st):
                pe.wait_ge(hT_copied, st.at(-2, 1, 1))
                for k in range(NT):
                    mm = t_.matmul(bank[7][:, 0:E], hT[:, k, :], rt_sb[:, k, :], start=(k == 0), stop=(k == NT - 1))
                mm.then_inc(lg_done, 1)

            pe.wait_ge(weights_in, 32)
            pe.wait_ge(router_in, 16)
            pe.wait_ge(consts_made, 10)
            s0 = Step(0, 0, RING, B, True)
            project_q(s0, 0)
            project_q(s0, 1)
            turn_values(s0, 0)

            def step(st):
                if st.has(2):
                    project_q(st, 2)
                if st.has(-1):
                    turn_max(st, -1, 1)
                for h in range(NH):
                    if h == 1 and st.has(-2):
                        turn_context(st)
                    if h == 2 and st.has(1):
                        turn_values(st, 1)
                    if h == 3 and st.has(-2):
                        project_out(st)
                    if h == 5 and st.has(-2):
                        turn_hidden(st)
                    if h == 6 and st.has(0):
                        turn_max(st, 0, 0)
                    if h == 7 and st.has(-2):
                        router(st)
                    if st.has(0):
                        scores_for_max(st, h)
                    if st.has(-1):
                        scores_for_exp(st, h)
                        if h >= 1:
                            apply_probs(st, h - 1)
                if st.has(-1):
                    apply_probs(st, NH - 1)

            attention_steps(pe, step)

            pe.wait_ge(onehot_made, 1)
            hot = onehot_b[:, :, :].rearrange("p b e -> p (b e)")
            t_.matmul(bank[0][:, 0:B * E], before[:, :], hot, start=True, stop=False)
            for d in range(1, B):
                mm = t_.matmul(bank[0][:, d * E:B * E], ones_b[:, :], hot[:, 0:(B - d) * E], start=False, stop=(d == B - 1))
            for b in range(B):
                mm = t_.matmul(bank[1][:, 0:E], ones_b[:, :], onehot_b[:, b, :], start=(b == 0), stop=(b == B - 1))
            mm.then_inc(ranks_done, 1)
            pe.wait_ge(cols_made, 1)
            for b in range(B):
                mm = t_.matmul(bank[2][:, 0:6 * NS], lo_hot[:, b, :], cols[:, b, :, :].rearrange("p a s -> p (a s)"),
                               start=(b == 0), stop=(b == B - 1))
            mm.then_inc(table_done, 1)

            pe.wait_ge(routed, 1)
            pe.wait_ge(experts_in, 64)

            def expert_of(st, d):
                m = st.at(d)
                return pe.value_load(expert_i[0:1, bass.ds(m, 1)], min_val=0, max_val=E - 1)

            def slot_step(st):
                if st.has(0):
                    c = st.slot(0)
                    pe.wait_ge(got_in[c], st.use(0, 16, 16))
                    if not st.first(0, 1):
                        pe.wait_ge(g_copied, st.at(0))
                    for k in range(NT):
                        mm = t_.transpose(bank[0][:, k * P:(k + 1) * P], got[c][:, k * P:(k + 1) * P], ident[:, :])
                    mm.then_inc(g_turned, 1)
                if st.has(-1):
                    m2 = (st.c - 1) % 2
                    e = expert_of(st, -1)
                    pe.wait_ge(g_copied, st.at(-1, 1, 1))
                    if not st.first(-1, 2):
                        pe.wait_ge(act_done, st.at(-1, 1, -1))
                    for k in range(NT):
                        mm = t_.matmul(bank[1 + m2][:, 0:I2], gotT[:, m2, k, :],
                                       gu_sb[:, k, bass.ds(e, 1), :].rearrange("p a i -> p (a i)"),
                                       start=(k == 0), stop=(k == NT - 1))
                    mm.then_inc(gu_done, 1)
                if st.has(-2):
                    m2 = (st.c - 2) % 2
                    pe.wait_ge(act_done, st.at(-2, 1, 1))
                    if not st.first(-2, 1):
                        pe.wait_ge(a_copied, st.at(-2))
                    t_.transpose(bank[3][:, 0:P], act_sb[:, m2, 0:P], ident[:, :])
                    t_.transpose(bank[3][0:IR, P:2 * P], act_sb[:, m2, P:I], ident[:, :]).then_inc(a_turned, 1)
                if st.has(-3):
                    m2 = (st.c - 3) % 2
                    e = expert_of(st, -3)
                    pe.wait_ge(a_copied, st.at(-3, 1, 1))
                    if not st.first(-3, 2):
                        pe.wait_ge(y_done, st.at(-3, 1, -1))
                    t_.matmul(bank[4 + m2][:, 0:T], actT[:, m2, 0, :],
                              dn_sb[:, bass.ds(e, 1), :].rearrange("p a t -> p (a t)"), start=True, stop=False)
                    t_.matmul(bank[4 + m2][:, 0:T], actT[0:IR, m2, 1, :],
                              dn2_sb[:, bass.ds(e, 1), :].rearrange("p a t -> p (a t)"),
                              start=False, stop=True).then_inc(dn_done, 1)

            expert_steps(pe, slot_step)

        @block.scalar
        def _(act):
            a = nc.scalar

            def copy_q(st, d):
                pe_b = bank[5][:, 0:T]
                act.wait_ge(q_done, st.at(d, 1, 1))
                if not st.first(d, RING):
                    act.wait_ge(parts_made, st.at(d - RING, 4, 4))
                    act.wait_ge(vt_done, st.at(d - RING, 1, 1))
                a.copy(q_sb[:, st.slot(d), :], pe_b).then_inc(q_copied, 1)

            def exponential(st, h):
                act.wait_ge(s2_done, st.at(-1, NH, h + 1))
                if h >= 2 or not st.first(-1, 1):
                    act.wait_ge(pv_done, st.at(-1, NH, h - 1))
                a.activation(probs[:, h % 2, :, :].rearrange("p k t -> p (k t)"), bank[2 + h % 2][:, 0:NT * T], ACT.Exp,
                             scale=float(DK) ** -0.5).then_inc(exp_done, 1)

            s0 = Step(0, 0, RING, B, True)
            copy_q(s0, 0)
            copy_q(s0, 1)

            def step(st):
                for h in range(NH):
                    if st.has(-1):
                        exponential(st, h)
                    if h == 0 and st.has(2):
                        copy_q(st, 2)
                    if h == 1 and st.has(-2):
                        act.wait_ge(ctxT_done, st.at(-2, 1, 1))
                        a.copy(ctxT[:, :], bank[7][:, 0:T]).then_inc(ctxT_copied, 1)
                    if h == 3 and st.has(-2):
                        act.wait_ge(h_done, st.at(-2, 1, 1))
                        if not st.first(-2, RING):
                            act.wait_ge(h_out[st.slot(-2)], st.use(-2, 16))
                        a.copy(h_sb[:, st.slot(-2), :], bank[7][:, 0:T]).then_inc(h_copied, 1)
                    if h == 5 and st.has(-2):
                        act.wait_ge(hT_done, st.at(-2, 1, 1))
                        a.copy(hT[:, :, :].rearrange("p k d -> p (k d)"), bank[7][:, 0:T]).then_inc(hT_copied, 1)
                    if h == 7 and st.has(-2):
                        act.wait_ge(lg_done, st.at(-2, 1, 1))
                        b = st.at(-2)
                        a.copy(logits[:, bass.ds(b, 1), :].rearrange("p a e -> p (a e)"), bank[7][:, 0:E]).then_inc(lg_copied, 1)

            attention_steps(act, step)
            act.wait_ge(gap_made, 1)
            a.activation(gate[:, :], gap[:, :], ACT.Exp).then_inc(gap_exp, 1)

            def slot_step(st):
                if st.has(0):
                    act.wait_ge(g_turned, st.at(0, 1, 1))
                    if not st.first(0, 2):
                        act.wait_ge(gu_done, st.at(0, 1, -1))
                    a.copy(gotT[:, st.c % 2, :, :].rearrange("p k s -> p (k s)"), bank[0][:, 0:2 * P]).then_inc(g_copied, 1)
                if st.has(-1):
                    m2 = (st.c - 1) % 2
                    act.wait_ge(gu_done, st.at(-1, 1, 1))
                    if not st.first(-1, 2):
                        act.wait_ge(act_done, st.at(-1, 1, -1))
                    a.activation(silu[:, m2, :], bank[1 + m2][:, 0:I], ACT.Silu).then_inc(silu_done, 1)
                if st.has(-2):
                    m2 = st.c % 2
                    act.wait_ge(a_turned, st.at(-2, 1, 1))
                    if not st.first(-2, 2):
                        act.wait_ge(dn_done, st.at(-2, 1, -1))
                    a.copy(actT[:, m2, 0, :], bank[3][:, 0:P])
                    a.copy(actT[0:IR, m2, 1, :], bank[3][0:IR, P:2 * P]).then_inc(a_copied, 1)

            expert_steps(act, slot_step)

        @block.vector
        def _(dve):
            v = nc.vector
            dve.wait_ge(cond_in, 16)
            v.tensor_scalar(mask2[:, 0, :], cond_sb[:, :], -NEG, NEG, ALU.mult, ALU.add).then_inc(bias_made, 1)
            v.tensor_copy(mask2[:, 1, :], cond_sb[:, :]).then_inc(bias_made, 1)
            dve.wait_ge(consts_made, 10)

            def copy_values(st, d):
                dve.wait_ge(vt_done, st.at(d, 1, 1))
                v.tensor_copy(v_sb[:, st.slot(d), :, :, 0:DK],
                              bank[6][:, 0:T].rearrange("p (k h c) -> p k h c", k=NT, h=NH)).then_inc(vt_copied, 1)

            def copy_max(st, d, half):
                dve.wait_ge(neg_turned, st.at(d, 2, half + 1))
                if not st.first(d, 1):
                    dve.wait_ge(max_in[half], st.at(d, 32))
                v.tensor_copy(neg_rows[:, half, :], bank[6][:, :].bitcast(BF16)[0:NH, 0:T]).then_inc(neg_copied, 1)

            def negate_max(st, half):
                dve.wait_ge(max_done, st.at(0, NH, 4 * half + 4))
                v.tensor_scalar(neg_max[:, half, :, 0, :], row_max[:, half, :, :], -1.0, None, ALU.mult).then_inc(neg_hi_made, 1)
                dve.wait_ge(neg_hi_made, st.at(0, 2, half + 1))
                v.scalar_tensor_tensor(out=neg_max[:, half, :, 1, :], in0=row_max[:, half, :, :], scalar=-1.0,
                                       in1=neg_max[:, half, :, 0, :], op0=ALU.mult, op1=ALU.subtract).then_inc(neg_made, 1)

            copy_values(Step(0, 0, RING, B, True), 0)

            def step(st):
                if st.has(-2):
                    dve.wait_ge(pv_done, st.at(-2, NH, NH))
                    pv = bank[4][:, 0:NT * NH * V1].rearrange("p (k h c) -> p k h c", k=NT, h=NH)
                    v.reciprocal(rsum[:, :, :], pv[:, :, :, DK]).then_inc(recip_done, 1)
                    dve.wait_ge(recip_done, st.at(-2, 1, 1))
                    if not st.first(-2, 1):
                        dve.wait_ge(ctxT_done, st.at(-2))
                    v.tensor_tensor(ctx_sb[:, :, :].rearrange("p k (h c) -> p (k h) c", h=NH),
                                    bank[4][:, 0:NT * NH * V1].rearrange("p (g c) -> p g c", c=V1)[:, :, 0:DK],
                                    rsum[:, :, :].rearrange("p k (h o) -> p (k h) o", o=1).to_broadcast([P, NT * NH, DK]), ALU.mult).then_inc(norm_done, 1)
                if st.has(-1):
                    copy_max(st, -1, 1)
                for h in range(NH):
                    if st.has(0):
                        dve.wait_ge(s1_done, st.at(0, NH, h + 1))
                        v.tensor_reduce(row_max[:, h // 4, :, h % 4:h % 4 + 1],
                                        bank[h % 2][:, 0:NT * T].rearrange("p (q k) -> p q k", q=NT), AX.X, ALU.max).then_inc(max_done, 1)
                    if h == 2 and st.has(1):
                        copy_values(st, 1)
                    if h == 3 and st.has(0):
                        negate_max(st, 0)
                    if h == 6 and st.has(0):
                        copy_max(st, 0, 0)
                if st.has(0):
                    negate_max(st, 1)

            attention_steps(dve, step)

            steps = [0]

            def then(ins):
                steps[0] += 1
                ins.then_inc(route_step, 1)
                dve.wait_ge(route_step, steps[0])

            dve.wait_ge(lg_copied, B)
            dve.wait_ge(iotas_made, 7)
            for b in range(B):
                last = v.max(out=top[:, b, :], in_=logits[:, b, :])
            then(last)
            v.tensor_tensor(gap[:, :], top[:, :, 1], top[:, :, 0], ALU.subtract).then_inc(gap_made, 1)
            best = top[:, :, 0:1].to_broadcast([P, B, E])
            then(v.tensor_tensor(picked[:, :, :], logits[:, :, :], best, ALU.is_equal))
            then(v.tensor_tensor(picked[:, :, :], picked[:, :, :], iota_e[:, :, :], ALU.mult))
            then(v.tensor_reduce(first[:, :], picked[:, :, :], AX.X, ALU.min))
            first_b = first[:, :].rearrange("p (b o) -> p b o", o=1).to_broadcast([P, B, E])
            then(v.tensor_tensor(onehot[:, :, :], iota_e[:, :, :], first_b, ALU.is_equal))
            v.tensor_copy(onehot_b[:, :, :], onehot[:, :, :]).then_inc(onehot_made, 1)
            dve.wait_ge(gap_exp, 1)
            then(v.tensor_scalar(gate[:, :], gate[:, :], 1.0, None, ALU.add))
            then(v.reciprocal(gate[:, :], gate[:, :]))
            then(v.tensor_copy(w_part[:, 0, :], gate[:, :]))
            then(v.tensor_tensor(w_rest[:, :], gate[:, :], w_part[:, 0, :], ALU.subtract))
            then(v.tensor_copy(w_part[:, 1, :], w_rest[:, :]))
            then(v.tensor_tensor(w_part[:, 2, :], w_rest[:, :], w_part[:, 1, :], ALU.subtract))
            dve.wait_ge(ranks_done, 1)
            then(v.tensor_copy(count[:, :], bank[1][:, 0:E]))
            then(v.tensor_tensor(filled[:, :, :], count[:, :].rearrange("p (e o) -> p e o", o=1).to_broadcast([P, E, B]),
                                 fill[:, :, :], ALU.is_gt))
            then(v.tensor_reduce(tiles[:, :], filled[:, :, :], AX.X, ALU.add))
            then(v.tensor_tensor_scan(tiles_to[:, :], one_e[:, :], tiles[:, :], 0.0, ALU.mult, ALU.add))
            then(v.tensor_tensor(start[:, :], tiles_to[:, :], tiles[:, :], ALU.subtract))
            start_b = start[:, :].rearrange("p (o e) -> p o e", o=1).to_broadcast([P, B, E])
            then(v.scalar_tensor_tensor(out=place[:, :, :], in0=start_b, scalar=float(P),
                                        in1=bank[0][:, 0:B * E].rearrange("p (b e) -> p b e", b=B), op0=ALU.mult, op1=ALU.add))
            then(v.tensor_tensor(place[:, :, :], place[:, :, :], onehot[:, :, :], ALU.mult))
            then(v.tensor_reduce(pos[:, :], place[:, :, :], AX.X, ALU.add))
            then(v.tensor_copy(pos_i[:, :], pos[:, :]))
            then(v.tensor_scalar(hi_i[:, :], pos_i[:, :], 7, None, ALU.logical_shift_right))
            then(v.tensor_scalar(lo_i[:, :], pos_i[:, :], P - 1, None, ALU.bitwise_and))
            then(v.tensor_copy(hi[:, :], hi_i[:, :]))
            then(v.tensor_copy(lo[:, :], lo_i[:, :]))
            for b in range(B):
                v.tensor_scalar(lo_hot[:, b, :], iota_col_b[:, :], lo[:, b:b + 1], None, ALU.is_equal)

            def per_token(ap):
                return ap.rearrange("p (b o) -> p b o", o=1).to_broadcast([P, B, NS])

            then(v.tensor_tensor(cols[:, :, 0, :], iota_s[:, :, :], per_token(hi[:, :]), ALU.is_equal))
            v.tensor_tensor(cols[:, :, 1, :], cols[:, :, 0, :], iota_b[:, :, :], ALU.mult)
            v.tensor_scalar(cols[:, :, 2, :], cols[:, :, 0, :], iota_p[:, 0:1], None, ALU.mult)
            for p in range(3):
                last = v.tensor_tensor(cols[:, :, 3 + p, :], cols[:, :, 0, :], per_token(w_part[:, p, :]), ALU.mult)
            last.then_inc(cols_made, 1)
            to_b = tiles_to[0:1, :].rearrange("p (o e) -> p o e", o=1).to_broadcast([1, NS, E])
            then(v.tensor_tensor(expert_cmp[:, :, :], tile_e[:, :, :], to_b, ALU.is_ge))
            then(v.tensor_reduce(expert_f[:, :], expert_cmp[:, :, :], AX.X, ALU.add))
            then(v.tensor_scalar(expert_i[:, :], expert_f[:, :], float(E - 1), None, ALU.min))
            dve.wait_ge(table_done, 1)
            then(v.tensor_copy(table[:, :, :].rearrange("p a s -> p (a s)"), bank[2][:, 0:6 * NS]))
            then(v.scalar_tensor_tensor(out=token[:, :], in0=table[:, 1, :], scalar=float(P), in1=table[:, 2, :],
                                        op0=ALU.mult, op1=ALU.add))
            v.tensor_copy(take_i[:, :], token[:, :]).then_inc(take_made, 1)
            then(v.tensor_scalar(token_f[:, :], table[:, 0, :], -float(TOK), float(TOK), ALU.mult, ALU.add))
            then(v.tensor_tensor(put_i[:, :], token_f[:, :], token[:, :], ALU.add))
            then(v.tensor_tensor(weight[:, :], table[:, 3, :], table[:, 4, :], ALU.add))
            v.tensor_tensor(weight[:, :], weight[:, :], table[:, 5, :], ALU.add).then_inc(routed, 1)
            dve.wait_ge(routed, 1)

            def slot_step(st):
                if st.has(-1):
                    m2 = (st.c - 1) % 2
                    dve.wait_ge(silu_done, st.at(-1, 1, 1))
                    if not st.first(-1, 2):
                        dve.wait_ge(a_turned, st.at(-1, 1, -1))
                    m = st.at(-1)
                    v.scalar_tensor_tensor(out=act_sb[:, m2, :], in0=silu[:, m2, :], scalar=weight[:, bass.ds(m, 1)],
                                           in1=bank[1 + m2][:, I:I2], op0=ALU.mult, op1=ALU.mult).then_inc(act_done, 1)
                if st.has(-3):
                    m2, c = (st.c - 3) % 2, st.slot(-3)
                    dve.wait_ge(dn_done, st.at(-3, 1, 1))
                    if not st.first(-3, SRING):
                        dve.wait_ge(y_out[c], st.use(-3, 16))
                    v.tensor_tensor(y_sb[c][:, :], bank[4 + m2][:, 0:T], got[c][:, T:2 * T], ALU.add).then_inc(y_done, 1)

            expert_steps(dve, slot_step)


def kernel(x, cond_2048, L0_cond_Wq, L0_cond_Wo, L0_ffn_router_w, L0_ffn_gate_w, L0_ffn_up_w, L0_ffn_down_w):
    import numpy as np
    import concourse.bacc as bacc
    from concourse import mybir as mb
    from concourse.bass_utils import run_bass_kernel_spmd as run

    data = {
        "x": x, "cond": cond_2048, "wqT": L0_cond_Wq.T, "woT": L0_cond_Wo.T, "routerT": L0_ffn_router_w.T,
        "guT": np.concatenate([L0_ffn_gate_w.transpose(0, 2, 1), L0_ffn_up_w.transpose(0, 2, 1)], axis=2),
        "dnT": L0_ffn_down_w.transpose(0, 2, 1),
    }
    nc = bacc.Bacc("TRN2", target_bir_lowering=False, num_devices=1)
    arrays, args = {}, []
    for name, a in data.items():
        a = np.ascontiguousarray(a)
        arrays[f"in_{name}"] = a
        args.append(nc.dram_tensor(f"in_{name}", a.shape, mb.dt.from_np(a.dtype), kind="ExternalInput").ap())
    args.append(nc.dram_tensor("out_0", x.shape, mb.dt.from_np(x.dtype), kind="ExternalOutput").ap())
    adaln_ffn(nc, *args)
    r = run(nc, [arrays], core_ids=[0])
    return r.results[0]["out_0"]
```

```python
from contextlib import ExitStack

import numpy as np

import concourse.bass as bass
from concourse import mybir

F32 = mybir.dt.float32
BF16 = mybir.dt.bfloat16
I32 = mybir.dt.int32
U32 = mybir.dt.uint32
ALU = mybir.AluOpType
ACT = mybir.ActivationFunctionType
AX = mybir.AxisListType

P = 128
NEG = -1e30
NH = 8
DK = P // NH
RING = 3
SRING = 6
LEFT = [0, 1, 2, 0, 1, 0]
RIGHT = [0, 0, 0, 1, 1, 2]
LEFT_RUNS = [(0, 0, 3), (3, 0, 2), (5, 0, 1)]
RIGHT_RUNS = [(0, 0, -3), (3, 1, -2), (5, 2, 1)]
ROW_MASK = len(LEFT) * DK
ROW_MAX = ROW_MASK + 1
ROWS1 = ROW_MASK + 1
ROWS2 = ROW_MAX + 2
STACK_DMAS = len(LEFT_RUNS) + len(RIGHT_RUNS) + 1


def adaln_ffn(nc, x, cond, wqT, woT, routerT, guT, dnT, out):
    B, D, T = x.shape
    E = routerT.shape[1]
    I2 = guT.shape[2]
    I = I2 // 2
    IR = I - P
    NT = T // P
    VC = 2 * DK
    HG = P // VC
    TOK = B * D
    SLOT_TILES = TOK // P + E - 1
    NS = SLOT_TILES
    assert D == P and NT == 2 and B == 16

    ctx = ExitStack()
    with ctx:
        def sb(name, shape, dt=F32):
            return ctx.enter_context(nc.sbuf_tensor(name, shape, dt))

        def sem(name):
            return ctx.enter_context(nc.semaphore(name))

        def sems(name, n):
            return [sem(f"{name}{i}") for i in range(n)]

        bank = [ctx.enter_context(nc.psum_tensor(f"bank{i}", [P, 512], F32)) for i in range(8)]

        parts_dram = [nc.dram_tensor(f"parts_dram{r}", [2, 3, P, T], BF16, kind="Internal").ap() for r in range(RING)]
        mask_dram = nc.dram_tensor("mask_dram", [B, 2, NH, T], BF16, kind="Internal").ap()
        rows_dram = nc.dram_tensor("rows_dram", [TOK, 2 * T], F32, kind="Internal").ap()

        ident = sb("ident", [P, P])
        ident_b = sb("ident_b", [P, P], BF16)
        before = sb("before", [P, P], BF16)
        ones_b = sb("ones_b", [P, P], BF16)
        iota_p = sb("iota_p", [P, 1])
        iota_col = sb("iota_col", [P, P])
        iota_col_b = sb("iota_col_b", [P, P], BF16)
        iota_e = sb("iota_e", [P, B, E])
        iota_b = sb("iota_b", [P, B, NS], BF16)
        iota_s = sb("iota_s", [P, B, NS])
        fill = sb("fill", [P, E, B])
        tile_e = sb("tile_e", [1, NS, E])

        wq_sb = sb("wq_sb", [P, P])
        wo_sb = sb("wo_sb", [P, P])
        rt_sb = sb("rt_sb", [P, NT, E])
        gu_sb = sb("gu_sb", [P, NT, E, I2])
        dn_sb = sb("dn_sb", [P, E, T])
        dn2_sb = sb("dn2_sb", [IR, E, T])

        cond_sb = sb("cond_sb", [B, T])
        mask2 = sb("mask2", [B, 2, T], BF16)
        cond_all = sb("cond_all", [P, B, T])
        x_sb = sb("x_sb", [P, B, T])
        q_sb = sb("q_sb", [P, RING, T])
        rest = sb("rest", [P, T])
        parts = sb("parts", [P, RING, 2, 3, T], BF16)
        stack = [sb(f"stack{r}", [P, 2, NH, T], BF16) for r in range(RING)]
        v_sb = sb("v_sb", [P, RING, NT, NH, VC])
        row_max = sb("row_max", [P, 2, NT, NH // 2])
        neg_max = sb("neg_max", [P, 2, NT, 2, NH // 2], BF16)
        neg_rows = sb("neg_rows", [NH, 2, T], BF16)
        probs = sb("probs", [P, NH, NT, T])
        pv_sb = sb("pv_sb", [P, NH // HG, T])
        rsum = sb("rsum", [P, NT * NH])
        ctx_sb = sb("ctx_sb", [P, NT, P])
        ctxT = sb("ctxT", [P, T])
        h_sb = sb("h_sb", [P, RING, T])
        hT = sb("hT", [P, NT, P])
        logits = sb("logits", [P, B, E])

        top = sb("top", [P, B, E])
        gap = sb("gap", [P, B])
        gate = sb("gate", [P, B])
        picked = sb("picked", [P, B, E])
        first = sb("first", [P, B])
        onehot = sb("onehot", [P, B, E])
        onehot_b = sb("onehot_b", [P, B, E], BF16)
        count = sb("count", [P, E])
        filled = sb("filled", [P, E, B])
        tiles = sb("tiles", [P, E])
        tiles_to = sb("tiles_to", [P, E])
        one_e = sb("one_e", [P, E])
        idle = sb("idle", [1, 128])
        start = sb("start", [P, E])
        place = sb("place", [P, B, E])
        pos = sb("pos", [P, B])
        pos_i = sb("pos_i", [P, B], I32)
        hi_i = sb("hi_i", [P, B], I32)
        lo_i = sb("lo_i", [P, B], I32)
        hi = sb("hi", [P, B])
        lo = sb("lo", [P, B])
        lo_hot = sb("lo_hot", [P, B, P], BF16)
        cols = sb("cols", [P, B, 6, NS], BF16)
        w_part = sb("w_part", [P, 3, B], BF16)
        w_rest = sb("w_rest", [P, B])
        table = sb("table", [P, 6, NS])
        token = sb("token", [P, NS])
        token_f = sb("token_f", [P, NS])
        take_i = sb("take_i", [P, NS], I32)
        put_i = sb("put_i", [P, NS], I32)
        weight = sb("weight", [P, NS])
        expert_cmp = sb("expert_cmp", [1, NS, E])
        expert_f = sb("expert_f", [1, NS])
        expert_i = sb("expert_i", [1, NS], I32)

        take = [sb(f"take{r}", [P, 1], I32) for r in range(SRING)]
        put = [sb(f"put{r}", [P, 1], I32) for r in range(SRING)]
        got = [sb(f"got{r}", [P, 2 * T]) for r in range(SRING)]
        gotT = sb("gotT", [P, 2, NT, P])
        silu = sb("silu", [P, 2, I])
        act_sb = sb("act_sb", [P, 2, I])
        actT = sb("actT", [P, 2, NT, P])
        y_sb = [sb(f"y_sb{r}", [P, T]) for r in range(SRING)]

        consts_made = sem("consts_made")
        iotas_made = sem("iotas_made")
        rows_made = sem("rows_made")
        cond_in = sem("cond_in")
        cond_all_in = sem("cond_all_in")
        weights_in = sem("weights_in")
        router_in = sem("router_in")
        experts_in = sem("experts_in")
        x_first_in = sem("x_first_in")
        x_rest_in = sem("x_rest_in")
        bias_made = sem("bias_made")
        mask_out = sem("mask_out")
        x_out = sem("x_out")
        q_done = sem("q_done")
        q_copied = sem("q_copied")
        parts_step = sem("parts_step")
        parts_made = sem("parts_made")
        parts_out = sems("parts_out", RING)
        stack_in = sems("stack_in", RING)
        vt_done = sem("vt_done")
        vt_copied = sem("vt_copied")
        s1_done = sem("s1_done")
        max_done = sem("max_done")
        neg_hi_made = sem("neg_hi_made")
        neg_made = sem("neg_made")
        neg_turned = sem("neg_turned")
        neg_copied = sem("neg_copied")
        max_in = sems("max_in", 2)
        s2_done = sem("s2_done")
        exp_done = sem("exp_done")
        pv_done = sem("pv_done")
        pv_copied = sem("pv_copied")
        pvT_done = sem("pvT_done")
        recip_done = sem("recip_done")
        norm_done = sem("norm_done")
        ctxT_done = sem("ctxT_done")
        ctxT_copied = sem("ctxT_copied")
        h_done = sem("h_done")
        h_copied = sem("h_copied")
        h_out = sems("h_out", RING)
        hT_done = sem("hT_done")
        hT_copied = sem("hT_copied")
        lg_done = sem("lg_done")
        lg_copied = sem("lg_copied")
        route_step = sem("route_step")
        gap_made = sem("gap_made")
        gap_exp = sem("gap_exp")
        onehot_made = sem("onehot_made")
        ranks_done = sem("ranks_done")
        cols_made = sem("cols_made")
        table_done = sem("table_done")
        take_made = sem("take_made")
        routed = sem("routed")
        took = sem("took")
        put_made = sem("put_made")
        got_in = sems("got_in", SRING)
        g_turned = sem("g_turned")
        g_copied = sem("g_copied")
        gu_done = sem("gu_done")
        silu_done = sem("silu_done")
        act_done = sem("act_done")
        a_turned = sem("a_turned")
        a_copied = sem("a_copied")
        dn_done = sem("dn_done")
        y_done = sem("y_done")
        y_out = sems("y_out", SRING)

        class Step:

            def __init__(self, c, j, n, items, peeled):
                self.c, self.j, self.n, self.items, self.peeled = c, j, n, items, peeled

            def has(self, d):
                return not self.peeled or 0 <= self.c + d < self.items

            def first(self, d, k):
                return self.peeled and self.c + d < k

            def at(self, d, times=1, plus=0):
                if self.peeled:
                    return times * (self.c + d) + plus
                return self.j * (self.n * times) + (times * (self.c + d) + plus)

            def slot(self, d):
                return (self.c + d) % self.n

            def use(self, d, times=1, plus=0):
                k = times * ((self.c + d) // self.n) + plus
                return k if self.peeled else self.j * times + k

        def run_steps(eng, step, n, items, first, loops, last):
            for c in range(first):
                step(Step(c, 0, n, items, True))
            with eng.Fori(0, loops) as j:
                for u in range(n):
                    step(Step(first + u, j, n, items, False))
            for c in range(first + n * loops, last):
                step(Step(c, 0, n, items, True))

        def attention_steps(eng, step):
            run_steps(eng, step, RING, B, 2, 4, B + 2)

        def expert_steps(eng, step):
            run_steps(eng, step, SRING, NS, 4, 3, NS + 3)

        block = ctx.enter_context(nc.Block())

        @block.gpsimd
        def _(pool):
            g = nc.gpsimd

            n_waits = [0]

            def wait_step(semaphore, value):
                pool.wait_ge(semaphore, value)
                if not isinstance(value, int):
                    n_waits[0] += 1
                    g.tensor_tensor(idle[:, n_waits[0]:n_waits[0] + 1], one_e[0:1, 0:1], one_e[0:1, 0:1], ALU.add)

            g.memset(ident[:, :], 0.0).then_inc(consts_made, 1)
            g.memset(before[:, :], 1.0).then_inc(consts_made, 1)
            g.memset(ones_b[:, :], 1.0).then_inc(consts_made, 1)
            pool.wait_ge(consts_made, 3)
            g.affine_select(out=ident[:, :], in_=ident[:, :], compare_op=ALU.not_equal, fill=1.0, base=0,
                            pattern=[[-1, P]], channel_multiplier=1).then_inc(consts_made, 1)
            g.affine_select(out=before[:, :], in_=before[:, :], compare_op=ALU.is_gt, fill=0.0, base=0,
                            pattern=[[1, P]], channel_multiplier=-1).then_inc(consts_made, 1)
            pool.wait_ge(consts_made, 5)
            g.tensor_copy(ident_b[:, :], ident[:, :]).then_inc(consts_made, 1)
            g.memset(one_e[:, :], 1.0).then_inc(consts_made, 1)
            pool.wait_ge(consts_made, 7)
            pool.wait_ge(cond_all_in, 32)

            def make_parts(st, d):
                k, pt = st.slot(d), parts[:, st.slot(d)]
                wait_step(q_copied, st.at(d, 1, 1))
                if not st.first(d, RING):
                    wait_step(parts_out[k], st.use(d, 16))
                g.tensor_copy(pt[:, 0, 0, :], q_sb[:, k, :]).then_inc(parts_step, 1)
                wait_step(parts_step, st.at(d, 3, 1))
                g.tensor_tensor(rest[:, :], q_sb[:, k, :], pt[:, 0, 0, :], ALU.subtract).then_inc(parts_step, 1)
                wait_step(parts_step, st.at(d, 3, 2))
                g.tensor_copy(pt[:, 0, 1, :], rest[:, :]).then_inc(parts_step, 1)
                wait_step(parts_step, st.at(d, 3, 3))
                g.tensor_tensor(pt[:, 0, 2, :], rest[:, :], pt[:, 0, 1, :], ALU.subtract).then_inc(parts_made, 1)
                wait_step(parts_made, st.at(d, 4, 1))
                b = st.at(d)
                mask = cond_all[:, bass.ds(b, 1), :].rearrange("p o t -> p (o t)")
                for p in range(3):
                    g.tensor_tensor(pt[:, 1, p, :], pt[:, 0, p, :], mask, ALU.mult).then_inc(parts_made, 1)

            make_parts(Step(0, 0, RING, B, True), 0)
            make_parts(Step(1, 0, RING, B, True), 0)

            def step(st):
                if st.has(2):
                    make_parts(st, 2)

            attention_steps(pool, step)

            def iota(ap, pattern, base=0, per_partition=0):
                g.iota(ap, pattern, base=base, channel_multiplier=per_partition,
                       allow_small_or_imprecise_dtypes=True).then_inc(iotas_made, 1)

            iota(iota_p[:, :], [[0, 1]], 0, 1)
            iota(iota_col_b[:, :], [[1, P]])
            iota(iota_e[:, :, :], [[0, B], [1, E]], -E)
            iota(iota_b[:, :, :], [[1, B], [0, NS]])
            iota(iota_s[:, :, :], [[0, B], [1, NS]])
            iota(fill[:, :, :], [[0, E], [P, B]])
            iota(tile_e[:, :, :], [[1, NS], [0, E]])

            for k in range(RING):
                pool.wait_ge(h_out[k], 16 * len(range(k, B, RING)))
            pool.wait_ge(x_out, 16)
            pool.wait_ge(take_made, 1)
            out_rows = out.rearrange("b d t -> (b d) t")

            def slot_step(st):
                c = st.slot(0)
                if st.has(-SRING):
                    wait_step(y_done, st.at(-SRING, 1, 1))
                    if not st.first(-SRING, SRING):
                        wait_step(y_out[c], st.use(-SRING, 16))
                    m = st.at(-SRING)
                    g.tensor_copy(put[c][:, :], put_i[:, bass.ds(m, 1)]).then_inc(put_made, 1)
                    wait_step(put_made, st.at(-SRING, 1, 1))
                    g.indirect_dma_start(out_rows, bass.IndirectOffsetOnAxis(ap=put[c][:, 0:1], axis=0),
                                         y_sb[c][:, :], None, bounds_check=TOK - 1,
                                         oob_is_err=False).then_inc(y_out[c], 16)
                if st.has(0):
                    if not st.first(0, SRING):
                        wait_step(got_in[c], st.use(0, 16))
                    n = st.at(0)
                    g.tensor_copy(take[c][:, :], take_i[:, bass.ds(n, 1)]).then_inc(took, 1)
                    wait_step(took, st.at(0, 1, 1))
                    g.indirect_dma_start(got[c][:, :], None, rows_dram[:, :],
                                         bass.IndirectOffsetOnAxis(ap=take[c][:, 0:1], axis=0)).then_inc(got_in[c], 16)

            run_steps(pool, slot_step, SRING, NS, SRING, 2, NS + SRING)
            for c in range(SRING):
                pool.wait_ge(y_out[c], 16 * len(range(c, NS, SRING)))

        @block.sync
        def _(sp):
            sp.dma_start(wq_sb[:, :], wqT).then_inc(weights_in, 16)
            sp.dma_start(x_sb[:, 0:2, :], x[0:2].rearrange("b d t -> d b t")).then_inc(x_first_in, 16)
            sp.dma_start(cond_sb[:, :], cond).then_inc(cond_in, 16)

            def load_cond(a, b):
                sp.dma_start(cond_all[:, a:b, :].rearrange("p b t -> p (b t)"),
                             cond[a:b, :].rearrange("(o b) t -> o (b t)", o=1).to_broadcast([P, (b - a) * T])).then_inc(cond_all_in, 16)

            load_cond(0, 2)
            sp.wait_ge(bias_made, 2)
            for side in range(2):
                sp.dma_start(mask_dram[:, side, :, :],
                             mask2[:, side:side + 1, :].to_broadcast([B, NH, T])).then_inc(mask_out, 16)
            load_cond(2, B)
            sp.dma_start(x_sb[:, 2:4, :], x[2:4].rearrange("b d t -> d b t")).then_inc(x_rest_in, 16)
            sp.dma_start(x_sb[:, 4:B, :], x[4:B].rearrange("b d t -> d b t")).then_inc(x_rest_in, 16)
            sp.dma_start(wo_sb[:, :], woT).then_inc(weights_in, 16)
            sp.dma_start(rt_sb[:, :, :], routerT.rearrange("(k p) e -> p k e", p=P)).then_inc(router_in, 16)

            def ready(st, *values):
                return values if st.peeled else [sp.snap(a) for a in values]

            def write_parts(st, d):
                k = st.slot(d)
                sp.wait_ge(parts_made, st.at(d, 4, 4))
                sp.dma_start(parts_dram[k].rearrange("s p r t -> r (s p) t"),
                             parts[:, k, :, :, :].rearrange("r s p t -> r (s p) t")).then_inc(parts_out[k], 16)

            def read_stack(st, d):
                k = st.slot(d)
                b, = ready(st, st.at(d))
                if not st.first(d, RING):
                    sp.wait_ge(s2_done, st.at(d - RING, NH, NH))
                sp.dma_start(stack[k][ROW_MASK:ROW_MASK + 1, :, :, :],
                             mask_dram[bass.ds(b, 1), :, :, :]).then_inc(stack_in[k], 16)
                sp.wait_ge(parts_out[k], st.use(d, 16, 16))
                for side, runs in enumerate((LEFT_RUNS, RIGHT_RUNS)):
                    for row, p, n in runs:
                        src = parts_dram[k][side, p:p + max(n, 1)].rearrange("p (k h) t -> p k (h t)", h=NH)
                        if n > 0:
                            src = src.rearrange("p k w -> (p k) w")
                        else:
                            src = src.to_broadcast([-n, DK, NH * T])
                        sp.dma_start(stack[k][row * DK:(row + abs(n)) * DK, side, :, :].rearrange("r h t -> r (h t)"),
                                     src).then_inc(stack_in[k], 16)

            def write_max(st, d, half):
                sp.wait_ge(neg_copied, st.at(d, 2, half + 1))
                n = NH // 2
                sp.dma_start(stack[st.slot(d)][ROW_MAX:ROW_MAX + 2, 1, half * n:half * n + n, :],
                             neg_rows[:, half, :]).then_inc(max_in[half], 16)

            write_parts(Step(0, 0, RING, B, True), 0)
            sp.wait_ge(mask_out, 32)
            sp.wait_ge(rows_made, RING)
            read_stack(Step(0, 0, RING, B, True), 0)
            write_parts(Step(1, 0, RING, B, True), 0)
            for k in range(NT):
                sp.dma_start(gu_sb[:, k, :, :], guT[:, k * P:(k + 1) * P, :].rearrange("e p i -> p e i")).then_inc(experts_in, 16)
            sp.dma_start(dn_sb[:, :, :], dnT[:, 0:P, :].rearrange("e i t -> i e t")).then_inc(experts_in, 16)
            sp.dma_start(dn2_sb[:, :, :], dnT[:, P:I, :].rearrange("e i t -> i e t")).then_inc(experts_in, 16)
            sp.dma_start(rows_dram[:, T:2 * T], x.rearrange("b d t -> (b d) t")).then_inc(x_out, 16)

            def step(st):
                if st.has(1):
                    read_stack(st, 1)
                if st.has(-1):
                    write_max(st, -1, 1)
                if st.has(2):
                    write_parts(st, 2)
                if st.has(-2):
                    t, copied = ready(st, st.at(-2, P), st.at(-2, 1, 1))
                    sp.wait_ge(h_copied, copied)
                    sp.dma_start(rows_dram[bass.ds(t, P), 0:T], h_sb[:, st.slot(-2), :]).then_inc(h_out[st.slot(-2)], 16)
                if st.has(0):
                    write_max(st, 0, 0)

            attention_steps(sp, step)

        @block.tensor
        def _(pe):
            t_ = nc.tensor

            def project_q(st, d):
                if st.first(d, 3):
                    pe.wait_ge(*((x_first_in, 16) if st.first(d, 2) else (x_rest_in, 32)))
                b = st.at(d)
                if not st.first(d, 1):
                    pe.wait_ge(q_copied, st.at(d))
                t_.matmul(bank[5][:, 0:T], wq_sb[:, :], x_sb[:, bass.ds(b, 1), :].rearrange("p o t -> p (o t)"), start=True, stop=True).then_inc(q_done, 1)

            def turn_values(st, d):
                pe.wait_ge(q_copied, st.at(d, 1, 1))
                if not st.first(d, 2):
                    pe.wait_ge(neg_copied, st.at(d - 2, 2, 2))
                elif not st.first(d, 1):
                    pe.wait_ge(vt_copied, 1)
                for k in range(NT):
                    mm = t_.transpose(bank[6][:, k * P:(k + 1) * P], q_sb[:, st.slot(d), k * P:(k + 1) * P], ident[:, :])
                mm.then_inc(vt_done, 1)

            def turn_max(st, d, half):
                pe.wait_ge(neg_made, st.at(d, 2, half + 1))
                last = d + (2 if half == 1 else 1)
                last = min(st.c + last, B) if st.peeled else st.at(last)
                pe.wait_ge(vt_copied, last if half == 1 else (min(st.c + d + 2, B) if st.peeled else st.at(d, 1, 2)))
                if half == 0 and not st.first(d, 1):
                    pe.wait_ge(neg_copied, st.at(d, 2))
                to = bank[6][:, :].bitcast(BF16)
                for q in range(NT):
                    mm = t_.transpose(to[0:NH, q * P:(q + 1) * P],
                                      neg_max[:, half, q, :, :].rearrange("p a h -> p (a h)"), ident_b[:, :])
                mm.then_inc(neg_turned, 1)

            def scores_for_max(st, h):
                k = st.slot(0)
                if h == 0:
                    pe.wait_ge(stack_in[k], st.use(0, 16 * STACK_DMAS, 16 * STACK_DMAS))
                if h >= 2 or not st.first(0, 1):
                    pe.wait_ge(max_done, st.at(0, NH, h - 1))
                for q in range(NT):
                    mm = t_.matmul(bank[h % 2][:, q * T:(q + 1) * T], stack[k][0:ROWS1, 1, h, q * P:(q + 1) * P],
                                   stack[k][0:ROWS1, 0, h, :], start=True, stop=True)
                mm.then_inc(s1_done, 1)

            def scores_for_exp(st, h):
                k = st.slot(-1)
                if h % 4 == 0:
                    pe.wait_ge(max_in[h // 4], st.at(-1, 16, 16))
                if h >= 2 or not st.first(-1, 1):
                    pe.wait_ge(exp_done, st.at(-1, NH, h - 1))
                for q in range(NT):
                    mm = t_.matmul(bank[2 + h % 2][:, q * T:(q + 1) * T], stack[k][0:ROWS2, 0, h, q * P:(q + 1) * P],
                                   stack[k][0:ROWS2, 1, h, :], start=True, stop=True)
                mm.then_inc(s2_done, 1)

            def apply_probs(st, d, g):
                pe.wait_ge(exp_done, st.at(d, NH, HG * (g + 1)))
                if g == 0:
                    if not st.first(d, 1):
                        pe.wait_ge(pv_copied, st.at(d))
                    pe.wait_ge(vt_copied, st.at(d, 1, 1))
                for k in range(NT):
                    for c in range(HG):
                        mm = t_.matmul(bank[4][c * VC:(c + 1) * VC, g * T:(g + 1) * T], v_sb[:, st.slot(d), k, HG * g + c, :],
                                       probs[:, HG * g + c, k, :], start=(k == 0), stop=(k == NT - 1))
                mm.then_inc(pv_done, 1)

            def turn_products(st):
                pe.wait_ge(pv_copied, st.at(-2, 1, 1))
                if not st.first(-2, 1):
                    pe.wait_ge(lg_copied, st.at(-2))
                for q in range(NT):
                    for g in range(NH // HG):
                        mm = t_.transpose(bank[7][:, (q * NT + g) * P:(q * NT + g + 1) * P],
                                          pv_sb[:, g, q * P:(q + 1) * P], ident[:, :])
                mm.then_inc(pvT_done, 1)

            def turn_context(st):
                pe.wait_ge(norm_done, st.at(-2, 1, 1))
                for k in range(NT):
                    mm = t_.transpose(bank[7][:, k * P:(k + 1) * P], ctx_sb[:, k, :], ident[:, :])
                mm.then_inc(ctxT_done, 1)

            def project_out(st):
                pe.wait_ge(ctxT_copied, st.at(-2, 1, 1))
                t_.matmul(bank[7][:, 0:T], wo_sb[:, :], ctxT[:, :], start=True, stop=True).then_inc(h_done, 1)

            def turn_hidden(st):
                pe.wait_ge(h_copied, st.at(-2, 1, 1))
                for k in range(NT):
                    mm = t_.transpose(bank[7][:, k * P:(k + 1) * P], h_sb[:, st.slot(-2), k * P:(k + 1) * P], ident[:, :])
                mm.then_inc(hT_done, 1)

            def router(st):
                pe.wait_ge(hT_copied, st.at(-2, 1, 1))
                for k in range(NT):
                    mm = t_.matmul(bank[7][:, 0:E], hT[:, k, :], rt_sb[:, k, :], start=(k == 0), stop=(k == NT - 1))
                mm.then_inc(lg_done, 1)

            pe.wait_ge(weights_in, 32)
            pe.wait_ge(router_in, 16)
            pe.wait_ge(consts_made, 7)
            s0 = Step(0, 0, RING, B, True)
            project_q(s0, 0)
            project_q(s0, 1)
            turn_values(s0, 0)

            def step(st):
                if st.has(2):
                    project_q(st, 2)
                if st.has(-1):
                    turn_max(st, -1, 1)
                for h in range(NH):
                    if h == 2 and st.has(-2):
                        turn_products(st)
                    if h == 3 and st.has(1):
                        turn_values(st, 1)
                    if h == 4 and st.has(-2):
                        turn_context(st)
                    if h == 5 and st.has(-2):
                        project_out(st)
                    if h == 6 and st.has(-2):
                        turn_hidden(st)
                    if h == 6 and st.has(0):
                        turn_max(st, 0, 0)
                    if h == 7 and st.has(-2):
                        router(st)
                    if st.has(0):
                        scores_for_max(st, h)
                    if st.has(-1):
                        scores_for_exp(st, h)
                    if h == 0 and st.has(-2):
                        apply_probs(st, -2, 1)
                    if h == 4 and st.has(-1):
                        apply_probs(st, -1, 0)

            attention_steps(pe, step)

            pe.wait_ge(onehot_made, 1)
            hot = onehot_b[:, :, :].rearrange("p b e -> p (b e)")
            t_.matmul(bank[0][:, 0:B * E], before[:, :], hot, start=True, stop=False)
            for d in range(1, B):
                mm = t_.matmul(bank[0][:, d * E:B * E], ones_b[:, :], hot[:, 0:(B - d) * E], start=False, stop=(d == B - 1))
            for b in range(B):
                mm = t_.matmul(bank[1][:, 0:E], ones_b[:, :], onehot_b[:, b, :], start=(b == 0), stop=(b == B - 1))
            mm.then_inc(ranks_done, 1)
            pe.wait_ge(cols_made, 1)
            for b in range(B):
                mm = t_.matmul(bank[2][:, 0:6 * NS], lo_hot[:, b, :], cols[:, b, :, :].rearrange("p a s -> p (a s)"),
                               start=(b == 0), stop=(b == B - 1))
            mm.then_inc(table_done, 1)

            pe.wait_ge(routed, 1)
            pe.wait_ge(experts_in, 64)

            def expert_of(st, d):
                m = st.at(d)
                return pe.value_load(expert_i[0:1, bass.ds(m, 1)], min_val=0, max_val=E - 1)

            def slot_step(st):
                if st.has(0):
                    c = st.slot(0)
                    pe.wait_ge(got_in[c], st.use(0, 16, 16))
                    if not st.first(0, 1):
                        pe.wait_ge(g_copied, st.at(0))
                    for k in range(NT):
                        mm = t_.transpose(bank[0][:, k * P:(k + 1) * P], got[c][:, k * P:(k + 1) * P], ident[:, :])
                    mm.then_inc(g_turned, 1)
                if st.has(-1):
                    m2 = (st.c - 1) % 2
                    e = expert_of(st, -1)
                    pe.wait_ge(g_copied, st.at(-1, 1, 1))
                    if not st.first(-1, 2):
                        pe.wait_ge(act_done, st.at(-1, 1, -1))
                    for k in range(NT):
                        mm = t_.matmul(bank[1 + m2][:, 0:I2], gotT[:, m2, k, :],
                                       gu_sb[:, k, bass.ds(e, 1), :].rearrange("p a i -> p (a i)"),
                                       start=(k == 0), stop=(k == NT - 1))
                    mm.then_inc(gu_done, 1)
                if st.has(-2):
                    m2 = (st.c - 2) % 2
                    pe.wait_ge(act_done, st.at(-2, 1, 1))
                    if not st.first(-2, 1):
                        pe.wait_ge(a_copied, st.at(-2))
                    t_.transpose(bank[3][:, 0:P], act_sb[:, m2, 0:P], ident[:, :])
                    t_.transpose(bank[3][0:IR, P:2 * P], act_sb[:, m2, P:I], ident[:, :]).then_inc(a_turned, 1)
                if st.has(-3):
                    m2 = (st.c - 3) % 2
                    e = expert_of(st, -3)
                    pe.wait_ge(a_copied, st.at(-3, 1, 1))
                    if not st.first(-3, 2):
                        pe.wait_ge(y_done, st.at(-3, 1, -1))
                    t_.matmul(bank[4 + m2][:, 0:T], actT[:, m2, 0, :],
                              dn_sb[:, bass.ds(e, 1), :].rearrange("p a t -> p (a t)"), start=True, stop=False)
                    t_.matmul(bank[4 + m2][:, 0:T], actT[0:IR, m2, 1, :],
                              dn2_sb[:, bass.ds(e, 1), :].rearrange("p a t -> p (a t)"),
                              start=False, stop=True).then_inc(dn_done, 1)

            expert_steps(pe, slot_step)

        @block.scalar
        def _(act):
            a = nc.scalar

            def copy_q(st, d):
                pe_b = bank[5][:, 0:T]
                act.wait_ge(q_done, st.at(d, 1, 1))
                if not st.first(d, RING):
                    act.wait_ge(parts_made, st.at(d - RING, 4, 4))
                    act.wait_ge(vt_done, st.at(d - RING, 1, 1))
                a.copy(q_sb[:, st.slot(d), :], pe_b).then_inc(q_copied, 1)

            def exponential(st, h):
                act.wait_ge(s2_done, st.at(-1, NH, h + 1))
                if h % HG == 0 and not st.first(-1, 1):
                    act.wait_ge(pv_done, st.at(-1, 2, h // HG - 1))
                a.activation(probs[:, h, :, :].rearrange("p k t -> p (k t)"), bank[2 + h % 2][:, 0:NT * T], ACT.Exp,
                             scale=float(DK) ** -0.5).then_inc(exp_done, 1)

            s0 = Step(0, 0, RING, B, True)
            copy_q(s0, 0)
            copy_q(s0, 1)

            def step(st):
                for h in range(NH):
                    if st.has(-1):
                        exponential(st, h)
                    if h == 0 and st.has(-2):
                        act.wait_ge(pv_done, st.at(-2, 2, 2))
                        if not st.first(-2, 1):
                            act.wait_ge(pvT_done, st.at(-2))
                        a.copy(pv_sb[:, :, :].rearrange("p g t -> p (g t)"), bank[4][:, :]).then_inc(pv_copied, 1)
                    if h == 1 and st.has(2):
                        copy_q(st, 2)
                    if h == 4 and st.has(-2):
                        act.wait_ge(ctxT_done, st.at(-2, 1, 1))
                        a.copy(ctxT[:, :], bank[7][:, 0:T]).then_inc(ctxT_copied, 1)
                    if h == 5 and st.has(-2):
                        act.wait_ge(h_done, st.at(-2, 1, 1))
                        if not st.first(-2, RING):
                            act.wait_ge(h_out[st.slot(-2)], st.use(-2, 16))
                        a.copy(h_sb[:, st.slot(-2), :], bank[7][:, 0:T]).then_inc(h_copied, 1)
                    if h == 6 and st.has(-2):
                        act.wait_ge(hT_done, st.at(-2, 1, 1))
                        a.copy(hT[:, :, :].rearrange("p k d -> p (k d)"), bank[7][:, 0:T]).then_inc(hT_copied, 1)
                    if h == 7 and st.has(-2):
                        act.wait_ge(lg_done, st.at(-2, 1, 1))
                        b = st.at(-2)
                        a.copy(logits[:, bass.ds(b, 1), :].rearrange("p a e -> p (a e)"), bank[7][:, 0:E]).then_inc(lg_copied, 1)

            attention_steps(act, step)
            act.wait_ge(gap_made, 1)
            a.activation(gate[:, :], gap[:, :], ACT.Exp).then_inc(gap_exp, 1)

            def slot_step(st):
                if st.has(0):
                    act.wait_ge(g_turned, st.at(0, 1, 1))
                    if not st.first(0, 2):
                        act.wait_ge(gu_done, st.at(0, 1, -1))
                    a.copy(gotT[:, st.c % 2, :, :].rearrange("p k s -> p (k s)"), bank[0][:, 0:2 * P]).then_inc(g_copied, 1)
                if st.has(-1):
                    m2 = (st.c - 1) % 2
                    act.wait_ge(gu_done, st.at(-1, 1, 1))
                    if not st.first(-1, 2):
                        act.wait_ge(act_done, st.at(-1, 1, -1))
                    a.activation(silu[:, m2, :], bank[1 + m2][:, 0:I], ACT.Silu).then_inc(silu_done, 1)
                if st.has(-2):
                    m2 = st.c % 2
                    act.wait_ge(a_turned, st.at(-2, 1, 1))
                    if not st.first(-2, 2):
                        act.wait_ge(dn_done, st.at(-2, 1, -1))
                    a.copy(actT[:, m2, 0, :], bank[3][:, 0:P])
                    a.copy(actT[0:IR, m2, 1, :], bank[3][0:IR, P:2 * P]).then_inc(a_copied, 1)

            expert_steps(act, slot_step)

        @block.vector
        def _(dve):
            v = nc.vector
            dve.wait_ge(cond_in, 16)
            v.tensor_scalar(mask2[:, 0, :], cond_sb[:, :], -NEG, NEG, ALU.mult, ALU.add).then_inc(bias_made, 1)
            v.tensor_copy(mask2[:, 1, :], cond_sb[:, :]).then_inc(bias_made, 1)
            ones_pair = float(np.frombuffer(np.array([0x3F803F80], np.uint32).tobytes(), np.float32)[0])
            for k in range(RING):
                v.memset(stack[k][ROW_MASK:P, 0, :, :].rearrange("p h t -> p (h t)").bitcast(F32), ones_pair).then_inc(rows_made, 1)
            v.memset(v_sb[:, :, :, :, :], 0.0).then_inc(rows_made, 1)
            dve.wait_ge(rows_made, RING + 1)
            v.memset(v_sb[:, :, :, :, DK:DK + 1], 1.0).then_inc(rows_made, 1)
            dve.wait_ge(rows_made, RING + 2)

            def copy_values(st, d):
                dve.wait_ge(vt_done, st.at(d, 1, 1))
                v.tensor_copy(v_sb[:, st.slot(d), :, :, 0:DK],
                              bank[6][:, 0:T].rearrange("p (k c h) -> p k h c", k=NT, h=NH)).then_inc(vt_copied, 1)

            def copy_max(st, d, half):
                dve.wait_ge(neg_turned, st.at(d, 2, half + 1))
                if not st.first(d, 1):
                    dve.wait_ge(max_in[half], st.at(d, 16))
                v.tensor_copy(neg_rows[:, half, :], bank[6][:, :].bitcast(BF16)[0:NH, 0:T]).then_inc(neg_copied, 1)

            def negate_max(st, half):
                dve.wait_ge(max_done, st.at(0, NH, 4 * half + 4))
                v.tensor_scalar(neg_max[:, half, :, 0, :], row_max[:, half, :, :], -1.0, None, ALU.mult).then_inc(neg_hi_made, 1)
                dve.wait_ge(neg_hi_made, st.at(0, 2, half + 1))
                v.scalar_tensor_tensor(out=neg_max[:, half, :, 1, :], in0=row_max[:, half, :, :], scalar=-1.0,
                                       in1=neg_max[:, half, :, 0, :], op0=ALU.mult, op1=ALU.subtract).then_inc(neg_made, 1)

            copy_values(Step(0, 0, RING, B, True), 0)

            def normalize(st):
                dve.wait_ge(pvT_done, st.at(-2, 1, 1))
                pv = bank[7][:, :].rearrange("p (g c) -> p g c", c=VC)
                v.reciprocal(rsum[:, :], pv[:, :, DK]).then_inc(recip_done, 1)
                dve.wait_ge(recip_done, st.at(-2, 1, 1))
                v.tensor_tensor(ctx_sb[:, :, :].rearrange("p k (h c) -> p (k h) c", h=NH), pv[:, :, 0:DK],
                                rsum[:, :].rearrange("p (g o) -> p g o", o=1).to_broadcast([P, NT * NH, DK]),
                                ALU.mult).then_inc(norm_done, 1)

            def step(st):
                for h in range(NH):
                    if st.has(0):
                        dve.wait_ge(s1_done, st.at(0, NH, h + 1))
                        v.tensor_reduce(row_max[:, h // 4, :, h % 4:h % 4 + 1],
                                        bank[h % 2][:, 0:NT * T].rearrange("p (q k) -> p q k", q=NT), AX.X, ALU.max).then_inc(max_done, 1)
                    if h == 0 and st.has(-1):
                        copy_max(st, -1, 1)
                    if h == 2 and st.has(-2):
                        normalize(st)
                    if h == 3 and st.has(1):
                        copy_values(st, 1)
                    if h == 3 and st.has(0):
                        negate_max(st, 0)
                    if h == 6 and st.has(0):
                        copy_max(st, 0, 0)
                if st.has(0):
                    negate_max(st, 1)

            attention_steps(dve, step)

            steps = [0]

            def then(ins):
                steps[0] += 1
                ins.then_inc(route_step, 1)
                dve.wait_ge(route_step, steps[0])

            dve.wait_ge(lg_copied, B)
            dve.wait_ge(iotas_made, 7)
            for b in range(B):
                last = v.max(out=top[:, b, :], in_=logits[:, b, :])
            then(last)
            v.tensor_tensor(gap[:, :], top[:, :, 1], top[:, :, 0], ALU.subtract).then_inc(gap_made, 1)
            best = top[:, :, 0:1].to_broadcast([P, B, E])
            then(v.tensor_tensor(picked[:, :, :], logits[:, :, :], best, ALU.is_equal))
            then(v.tensor_tensor(picked[:, :, :], picked[:, :, :], iota_e[:, :, :], ALU.mult))
            then(v.tensor_reduce(first[:, :], picked[:, :, :], AX.X, ALU.min))
            first_b = first[:, :].rearrange("p (b o) -> p b o", o=1).to_broadcast([P, B, E])
            then(v.tensor_tensor(onehot[:, :, :], iota_e[:, :, :], first_b, ALU.is_equal))
            v.tensor_copy(onehot_b[:, :, :], onehot[:, :, :]).then_inc(onehot_made, 1)
            dve.wait_ge(gap_exp, 1)
            then(v.tensor_scalar(gate[:, :], gate[:, :], 1.0, None, ALU.add))
            then(v.reciprocal(gate[:, :], gate[:, :]))
            then(v.tensor_copy(w_part[:, 0, :], gate[:, :]))
            then(v.tensor_tensor(w_rest[:, :], gate[:, :], w_part[:, 0, :], ALU.subtract))
            then(v.tensor_copy(w_part[:, 1, :], w_rest[:, :]))
            then(v.tensor_tensor(w_part[:, 2, :], w_rest[:, :], w_part[:, 1, :], ALU.subtract))
            dve.wait_ge(ranks_done, 1)
            then(v.tensor_copy(count[:, :], bank[1][:, 0:E]))
            then(v.tensor_tensor(filled[:, :, :], count[:, :].rearrange("p (e o) -> p e o", o=1).to_broadcast([P, E, B]),
                                 fill[:, :, :], ALU.is_gt))
            then(v.tensor_reduce(tiles[:, :], filled[:, :, :], AX.X, ALU.add))
            then(v.tensor_tensor_scan(tiles_to[:, :], one_e[:, :], tiles[:, :], 0.0, ALU.mult, ALU.add))
            then(v.tensor_tensor(start[:, :], tiles_to[:, :], tiles[:, :], ALU.subtract))
            start_b = start[:, :].rearrange("p (o e) -> p o e", o=1).to_broadcast([P, B, E])
            then(v.scalar_tensor_tensor(out=place[:, :, :], in0=start_b, scalar=float(P),
                                        in1=bank[0][:, 0:B * E].rearrange("p (b e) -> p b e", b=B), op0=ALU.mult, op1=ALU.add))
            then(v.tensor_tensor(place[:, :, :], place[:, :, :], onehot[:, :, :], ALU.mult))
            then(v.tensor_reduce(pos[:, :], place[:, :, :], AX.X, ALU.add))
            then(v.tensor_copy(pos_i[:, :], pos[:, :]))
            then(v.tensor_scalar(hi_i[:, :], pos_i[:, :], 7, None, ALU.logical_shift_right))
            then(v.tensor_scalar(lo_i[:, :], pos_i[:, :], P - 1, None, ALU.bitwise_and))
            then(v.tensor_copy(hi[:, :], hi_i[:, :]))
            then(v.tensor_copy(lo[:, :], lo_i[:, :]))
            for b in range(B):
                v.tensor_scalar(lo_hot[:, b, :], iota_col_b[:, :], lo[:, b:b + 1], None, ALU.is_equal)

            def per_token(ap):
                return ap.rearrange("p (b o) -> p b o", o=1).to_broadcast([P, B, NS])

            then(v.tensor_tensor(cols[:, :, 0, :], iota_s[:, :, :], per_token(hi[:, :]), ALU.is_equal))
            v.tensor_tensor(cols[:, :, 1, :], cols[:, :, 0, :], iota_b[:, :, :], ALU.mult)
            v.tensor_scalar(cols[:, :, 2, :], cols[:, :, 0, :], iota_p[:, 0:1], None, ALU.mult)
            for p in range(3):
                last = v.tensor_tensor(cols[:, :, 3 + p, :], cols[:, :, 0, :], per_token(w_part[:, p, :]), ALU.mult)
            last.then_inc(cols_made, 1)
            to_b = tiles_to[0:1, :].rearrange("p (o e) -> p o e", o=1).to_broadcast([1, NS, E])
            then(v.tensor_tensor(expert_cmp[:, :, :], tile_e[:, :, :], to_b, ALU.is_ge))
            then(v.tensor_reduce(expert_f[:, :], expert_cmp[:, :, :], AX.X, ALU.add))
            then(v.tensor_scalar(expert_i[:, :], expert_f[:, :], float(E - 1), None, ALU.min))
            dve.wait_ge(table_done, 1)
            then(v.tensor_copy(table[:, :, :].rearrange("p a s -> p (a s)"), bank[2][:, 0:6 * NS]))
            then(v.scalar_tensor_tensor(out=token[:, :], in0=table[:, 1, :], scalar=float(P), in1=table[:, 2, :],
                                        op0=ALU.mult, op1=ALU.add))
            v.tensor_copy(take_i[:, :], token[:, :]).then_inc(take_made, 1)
            then(v.tensor_scalar(token_f[:, :], table[:, 0, :], -float(TOK), float(TOK), ALU.mult, ALU.add))
            then(v.tensor_tensor(put_i[:, :], token_f[:, :], token[:, :], ALU.add))
            then(v.tensor_tensor(weight[:, :], table[:, 3, :], table[:, 4, :], ALU.add))
            v.tensor_tensor(weight[:, :], weight[:, :], table[:, 5, :], ALU.add).then_inc(routed, 1)
            dve.wait_ge(routed, 1)

            def slot_step(st):
                if st.has(-1):
                    m2 = (st.c - 1) % 2
                    dve.wait_ge(silu_done, st.at(-1, 1, 1))
                    if not st.first(-1, 2):
                        dve.wait_ge(a_turned, st.at(-1, 1, -1))
                    m = st.at(-1)
                    v.scalar_tensor_tensor(out=act_sb[:, m2, :], in0=silu[:, m2, :], scalar=weight[:, bass.ds(m, 1)],
                                           in1=bank[1 + m2][:, I:I2], op0=ALU.mult, op1=ALU.mult).then_inc(act_done, 1)
                if st.has(-3):
                    m2, c = (st.c - 3) % 2, st.slot(-3)
                    dve.wait_ge(dn_done, st.at(-3, 1, 1))
                    if not st.first(-3, SRING):
                        dve.wait_ge(y_out[c], st.use(-3, 16))
                    v.tensor_tensor(y_sb[c][:, :], bank[4 + m2][:, 0:T], got[c][:, T:2 * T], ALU.add).then_inc(y_done, 1)

            expert_steps(dve, slot_step)


def kernel(x, cond_2048, L0_cond_Wq, L0_cond_Wo, L0_ffn_router_w, L0_ffn_gate_w, L0_ffn_up_w, L0_ffn_down_w):
    import numpy as np
    import concourse.bacc as bacc
    from concourse import mybir as mb
    from concourse.bass_utils import run_bass_kernel_spmd as run

    dk = L0_cond_Wq.shape[0] // NH
    wqT = np.asarray(L0_cond_Wq).reshape(NH, dk, -1).transpose(2, 1, 0).reshape(-1, NH * dk)
    data = {
        "x": x, "cond": cond_2048, "wqT": wqT, "woT": L0_cond_Wo.T, "routerT": L0_ffn_router_w.T,
        "guT": np.concatenate([L0_ffn_gate_w.transpose(0, 2, 1), L0_ffn_up_w.transpose(0, 2, 1)], axis=2),
        "dnT": L0_ffn_down_w.transpose(0, 2, 1),
    }
    nc = bacc.Bacc("TRN2", target_bir_lowering=False, num_devices=1)
    arrays, args = {}, []
    for name, a in data.items():
        a = np.ascontiguousarray(a)
        arrays[f"in_{name}"] = a
        args.append(nc.dram_tensor(f"in_{name}", a.shape, mb.dt.from_np(a.dtype), kind="ExternalInput").ap())
    args.append(nc.dram_tensor("out_0", x.shape, mb.dt.from_np(x.dtype), kind="ExternalOutput").ap())
    adaln_ffn(nc, *args)
    r = run(nc, [arrays], core_ids=[0])
    return r.results[0]["out_0"]
```

```python
from contextlib import ExitStack

import numpy as np

import concourse.bass as bass
from concourse import mybir

F32 = mybir.dt.float32
BF16 = mybir.dt.bfloat16
I32 = mybir.dt.int32
U32 = mybir.dt.uint32
ALU = mybir.AluOpType
ACT = mybir.ActivationFunctionType
AX = mybir.AxisListType

P = 128
NEG = -1e30
NH = 8
DK = P // NH
RING = 3
SRING = 6
LEFT = [0, 1, 2, 0, 1, 0]
RIGHT = [0, 0, 0, 1, 1, 2]
LEFT_RUNS = [(0, 0, 3), (3, 0, 2), (5, 0, 1)]
RIGHT_RUNS = [(0, 0, -3), (3, 1, -2), (5, 2, 1)]
ROW_MASK = len(LEFT) * DK
ROW_MAX = ROW_MASK + 1
ROWS1 = ROW_MASK + 1
ROWS2 = ROW_MAX + 2
STACK_DMAS = len(LEFT_RUNS) + len(RIGHT_RUNS) + 1


def adaln_ffn(nc, x, cond, wqT, woT, routerT, guT, dnT, out):
    B, D, T = x.shape
    E = routerT.shape[1]
    I2 = guT.shape[2]
    I = I2 // 2
    IR = I - P
    NT = T // P
    VC = 2 * DK
    HG = P // VC
    TOK = B * D
    SLOT_TILES = TOK // P + E - 1
    NS = SLOT_TILES
    ROW = 2 * T + 1
    HOT = 11
    assert D == P and NT == 2 and B == 16

    ctx = ExitStack()
    with ctx:
        def sb(name, shape, dt=F32):
            return ctx.enter_context(nc.sbuf_tensor(name, shape, dt))

        def sem(name):
            return ctx.enter_context(nc.semaphore(name))

        def sems(name, n):
            return [sem(f"{name}{i}") for i in range(n)]

        bank = [ctx.enter_context(nc.psum_tensor(f"bank{i}", [P, 512], F32)) for i in range(8)]

        parts_dram = [nc.dram_tensor(f"parts_dram{r}", [2, 3, P, T], BF16, kind="Internal").ap() for r in range(RING)]
        mask_dram = nc.dram_tensor("mask_dram", [B, 2, NH, T], BF16, kind="Internal").ap()
        rows_dram = nc.dram_tensor("rows_dram", [TOK, ROW], F32, kind="Internal").ap()

        ident = sb("ident", [P, P])
        ident_b = sb("ident_b", [P, P], BF16)
        before = sb("before", [P, P], BF16)
        ones_b = sb("ones_b", [P, P], BF16)
        iota_col = sb("iota_col", [P, P], BF16)
        iota_e = sb("iota_e", [P, E], U32)
        iota_p = sb("iota_p", [P, B, NS], BF16)
        iota_b = sb("iota_b", [P, B, NS], BF16)
        iota_s = sb("iota_s", [P, B, NS], BF16)
        fill = sb("fill", [P, E, B])
        tile_e = sb("tile_e", [1, NS, E])

        wq_sb = sb("wq_sb", [P, P])
        wo_sb = sb("wo_sb", [P, P])
        rt_sb = sb("rt_sb", [P, NT, E])
        gu_sb = sb("gu_sb", [P, NT, E, I2])
        dn_sb = sb("dn_sb", [P, E, T])
        dn2_sb = sb("dn2_sb", [IR, E, T])

        cond_sb = sb("cond_sb", [B, T])
        mask2 = sb("mask2", [B, 2, T], BF16)
        cond_all = sb("cond_all", [P, B, T])
        x_sb = sb("x_sb", [P, B, T])
        q_sb = sb("q_sb", [P, RING, T])
        rest = sb("rest", [P, T])
        first_rest = sb("first_rest", [P, T])
        parts = sb("parts", [P, RING, 2, 3, T], BF16)
        stack = [sb(f"stack{r}", [P, 2, NH, T], BF16) for r in range(RING)]
        v_sb = sb("v_sb", [P, RING, NT, NH, VC])
        row_max = sb("row_max", [P, 2, NT, NH // 2])
        neg_max = sb("neg_max", [P, 2, NT, 2, NH // 2], BF16)
        neg_rows = sb("neg_rows", [NH, 2, T], BF16)
        probs = sb("probs", [P, NH, NT, T])
        pv_sb = sb("pv_sb", [P, NH // HG, T])
        rsum = sb("rsum", [P, NT * NH])
        ctx_sb = sb("ctx_sb", [P, NT, P])
        ctxT = sb("ctxT", [P, T])
        h_sb = sb("h_sb", [P, RING, T])
        hT = sb("hT", [P, NT, P])
        logits = sb("logits", [P, RING, E])

        top = sb("top", [P, RING, E])
        best = sb("best", [P, RING, E], U32)
        gap = sb("gap", [P, B])
        gate = sb("gate", [P, B])
        onehot = sb("onehot", [P, B, E], BF16)
        earlier = sb("earlier", [P, B + 1, E], BF16)
        filled = sb("filled", [P, E, B])
        tiles = sb("tiles", [P, E])
        tiles_to = sb("tiles_to", [P, E])
        one_e = sb("one_e", [P, E])
        idle = sb("idle", [1, 128])
        start = sb("start", [P, E])
        start_of = sb("start_of", [P, B, E])
        first_tile = sb("first_tile", [P, B])
        rank_of = sb("rank_of", [P, B, E])
        rank = sb("rank", [P, B])
        rank_i = sb("rank_i", [P, B], I32)
        hi_i = sb("hi_i", [P, B], I32)
        lo_i = sb("lo_i", [P, B], I32)
        rank_hi = sb("rank_hi", [P, B])
        hi = sb("hi", [P, B])
        lo = sb("lo", [P, B])
        lo_hot = sb("lo_hot", [P, B, P], BF16)
        hi_hot = sb("hi_hot", [P, B, NS], BF16)
        cols = sb("cols", [P, B, 2, NS], BF16)
        table = sb("table", [P, NS])
        token = sb("token", [P, NS])
        empty = sb("empty", [P, NS])
        take_i = sb("take_i", [P, NS], I32)
        put_i = sb("put_i", [P, NS], I32)
        expert_cmp = sb("expert_cmp", [1, NS, E])
        expert_f = sb("expert_f", [1, NS])
        expert_i = sb("expert_i", [1, NS], I32)

        got = [sb(f"got{r}", [P, ROW]) for r in range(SRING)]
        gotT = sb("gotT", [P, 2, NT, P])
        silu = sb("silu", [P, 2, I])
        act_sb = sb("act_sb", [P, 2, I])
        actT = sb("actT", [P, 2, NT, P])
        y_sb = [sb(f"y_sb{r}", [P, T]) for r in range(SRING)]

        consts_made = sem("consts_made")
        iotas_made = sem("iotas_made")
        rows_made = sem("rows_made")
        values_made = sem("values_made")
        cond_in = sem("cond_in")
        cond_all_in = sems("cond_all_in", RING)
        wq_in = sem("wq_in")
        wo_in = sem("wo_in")
        router_in = sem("router_in")
        experts_in = sem("experts_in")
        x_in = sems("x_in", RING)
        bias_made = sem("bias_made")
        mask_out = sem("mask_out")
        x_out = sem("x_out")
        q_done = sem("q_done")
        q_copied = sem("q_copied")
        parts_step = sem("parts_step")
        parts_made = sem("parts_made")
        parts_out = sems("parts_out", RING)
        stack_in = sems("stack_in", RING)
        vt_done = sem("vt_done")
        vt_copied = sem("vt_copied")
        s1_done = sem("s1_done")
        max_done = sem("max_done")
        neg_hi_made = sem("neg_hi_made")
        neg_made = sem("neg_made")
        neg_turned = sem("neg_turned")
        neg_copied = sem("neg_copied")
        max_in = sems("max_in", 2)
        s2_done = sem("s2_done")
        exp_done = sem("exp_done")
        pv_done = sem("pv_done")
        pv_copied = sem("pv_copied")
        pvT_done = sem("pvT_done")
        recip_done = sem("recip_done")
        norm_done = sem("norm_done")
        ctxT_done = sem("ctxT_done")
        ctxT_copied = sem("ctxT_copied")
        h_done = sem("h_done")
        h_copied = sem("h_copied")
        h_out = sems("h_out", RING)
        hT_done = sem("hT_done")
        hT_copied = sem("hT_copied")
        lg_done = sem("lg_done")
        lg_copied = sem("lg_copied")
        best_made = sem("best_made")
        top_made = sem("top_made")
        onehot_made = sem("onehot_made")
        added = sem("added")
        route_step = sem("route_step")
        gap_exp = sem("gap_exp")
        gate_made = sem("gate_made")
        gate_out = sem("gate_out")
        ranks_done = sem("ranks_done")
        cols_made = sem("cols_made")
        lo_made = sem("lo_made")
        lo_hot_made = sem("lo_hot_made")
        rest_hot_made = sem("rest_hot_made")
        table_done = sem("table_done")
        take_made = sem("take_made")
        put_made = sem("put_made")
        experts_found = sem("experts_found")
        got_in = sems("got_in", SRING)
        g_turned = sem("g_turned")
        g_copied = sem("g_copied")
        gu_done = sem("gu_done")
        silu_done = sem("silu_done")
        act_done = sem("act_done")
        a_turned = sem("a_turned")
        a_copied = sem("a_copied")
        dn_done = sem("dn_done")
        y_done = sem("y_done")
        y_out = sems("y_out", SRING)

        class Step:

            def __init__(self, c, j, n, items, peeled):
                self.c, self.j, self.n, self.items, self.peeled = c, j, n, items, peeled

            def has(self, d):
                return not self.peeled or 0 <= self.c + d < self.items

            def first(self, d, k):
                return self.peeled and self.c + d < k

            def at(self, d, times=1, plus=0):
                if self.peeled:
                    return times * (self.c + d) + plus
                return self.j * (self.n * times) + (times * (self.c + d) + plus)

            def slot(self, d):
                return (self.c + d) % self.n

            def use(self, d, times=1, plus=0):
                k = times * ((self.c + d) // self.n) + plus
                return k if self.peeled else self.j * times + k

        def run_steps(eng, step, n, items, first, loops, last):
            for c in range(first):
                step(Step(c, 0, n, items, True))
            with eng.Fori(0, loops) as j:
                for u in range(n):
                    step(Step(first + u, j, n, items, False))
            for c in range(first + n * loops, last):
                step(Step(c, 0, n, items, True))

        def attention_steps(eng, step):
            run_steps(eng, step, RING, B, 3, 3, B + 3)

        def expert_steps(eng, step):
            run_steps(eng, step, SRING, NS, 4, 3, NS + 3)

        block = ctx.enter_context(nc.Block())

        @block.gpsimd
        def _(pool):
            g = nc.gpsimd

            n_waits = [0]

            def wait_step(semaphore, value):
                pool.wait_ge(semaphore, value)
                if not isinstance(value, int):
                    n_waits[0] += 1
                    g.tensor_tensor(idle[:, n_waits[0]:n_waits[0] + 1], one_e[0:1, 0:1], one_e[0:1, 0:1], ALU.add)

            g.memset(ident[:, :], 0.0).then_inc(consts_made, 1)
            g.memset(before[:, :], 1.0).then_inc(consts_made, 1)
            g.memset(ones_b[:, :], 1.0).then_inc(consts_made, 1)
            pool.wait_ge(consts_made, 3)
            g.affine_select(out=ident[:, :], in_=ident[:, :], compare_op=ALU.not_equal, fill=1.0, base=0,
                            pattern=[[-1, P]], channel_multiplier=1).then_inc(consts_made, 1)
            g.affine_select(out=before[:, :], in_=before[:, :], compare_op=ALU.is_gt, fill=0.0, base=0,
                            pattern=[[1, P]], channel_multiplier=-1).then_inc(consts_made, 1)
            pool.wait_ge(consts_made, 5)
            g.tensor_copy(ident_b[:, :], ident[:, :]).then_inc(consts_made, 1)
            g.memset(v_sb[:, :, :, :, :], 0.0).then_inc(values_made, 1)
            pool.wait_ge(values_made, 1)
            g.memset(v_sb[:, :, :, :, DK:DK + 1], 1.0).then_inc(values_made, 1)
            g.memset(one_e[:, :], 1.0).then_inc(consts_made, 1)
            pool.wait_ge(consts_made, 7)

            def make_parts(st, d):
                k, pt = st.slot(d), parts[:, st.slot(d)]
                wait_step(cond_all_in[k], st.use(d, 16, 16))
                wait_step(q_copied, st.at(d, 1, 1))
                g.tensor_tensor(pt[:, 0, 1, :], q_sb[:, k, :], pt[:, 0, 0, :], ALU.subtract)
                g.tensor_tensor(rest[:, :], q_sb[:, k, :], pt[:, 0, 0, :], ALU.subtract).then_inc(parts_step, 1)
                wait_step(parts_step, st.at(d, 1, 1))
                g.tensor_tensor(pt[:, 0, 2, :], rest[:, :], pt[:, 0, 1, :], ALU.subtract).then_inc(parts_made, 1)
                wait_step(parts_made, st.at(d, 4, 1))
                b = st.at(d)
                mask = cond_all[:, bass.ds(b, 1), :].rearrange("p o t -> p (o t)")
                for p in range(3):
                    g.tensor_tensor(pt[:, 1, p, :], pt[:, 0, p, :], mask, ALU.mult).then_inc(parts_made, 1)

            def iota(ap, pattern, base=0, per_partition=0):
                g.iota(ap, pattern, base=base, channel_multiplier=per_partition,
                       allow_small_or_imprecise_dtypes=True).then_inc(iotas_made, 1)

            g.memset(earlier[:, 0, :], 0.0).then_inc(iotas_made, 1)
            iota(iota_e[:, :], [[1, E]])
            iota(iota_col[:, :], [[1, P]])
            iota(iota_p[:, :, :], [[0, B], [0, NS]], 0, 1)
            iota(iota_b[:, :, :], [[1, B], [0, NS]], 1)
            iota(iota_s[:, :, :], [[0, B], [1, NS]])
            iota(fill[:, :, :], [[0, E], [P, B]])
            iota(tile_e[:, :, :], [[1, NS], [0, E]])
            pool.wait_ge(iotas_made, 8)
            pool.wait_ge(parts_made, 4)
            make_parts(Step(1, 0, RING, B, True), 0)

            def add_tokens(st):
                b = st.at(-3)
                hot = onehot[:, bass.ds(b, 1), :].rearrange("p a e -> p (a e)")
                wait_step(onehot_made, st.at(-3, 1, 1))
                if not st.first(-3, 1):
                    wait_step(added, st.at(-3))
                after = st.at(-3, 1, 1)
                g.tensor_tensor(earlier[:, bass.ds(after, 1), :].rearrange("p a e -> p (a e)"),
                                earlier[:, bass.ds(b, 1), :].rearrange("p a e -> p (a e)"), hot, ALU.add).then_inc(added, 1)

            def step(st):
                if st.has(2):
                    make_parts(st, 2)
                if st.has(-3):
                    add_tokens(st)

            attention_steps(pool, step)

            pool.wait_ge(lo_made, 1)
            for b in range(HOT, B):
                g.tensor_scalar(lo_hot[:, b, :], iota_col[:, :], lo[:, b:b + 1], None, ALU.is_equal).then_inc(rest_hot_made, 1)

            for k in range(RING):
                pool.wait_ge(h_out[k], 16 * len(range(k, B, RING)))
            pool.wait_ge(x_out, 16 * B)
            pool.wait_ge(gate_out, 16)
            pool.wait_ge(take_made, 1)
            out_rows = out.rearrange("b d t -> (b d) t")

            for n in range(NS + SRING):
                c, m = n % SRING, n - SRING
                if m >= 0:
                    pool.wait_ge(y_done, m + 1)
                    if m == 0:
                        pool.wait_ge(put_made, 1)
                    g.indirect_dma_start(out_rows, bass.IndirectOffsetOnAxis(ap=put_i[:, m:m + 1], axis=0),
                                         y_sb[c][:, :], None, bounds_check=TOK - 1,
                                         oob_is_err=False).then_inc(y_out[c], 16)
                if n < NS:
                    g.indirect_dma_start(got[c][:, :], None, rows_dram[:, :],
                                         bass.IndirectOffsetOnAxis(ap=take_i[:, n:n + 1], axis=0)).then_inc(got_in[c], 16)
            for c in range(SRING):
                pool.wait_ge(y_out[c], 16 * len(range(c, NS, SRING)))

        @block.sync
        def _(sp):
            sp.dma_start(wq_sb[:, :], wqT).then_inc(wq_in, 16)
            def ready(st, *values):
                return values if st.peeled else [sp.snap(a) for a in values]

            def load_x(st, d):
                b, = ready(st, st.at(d))
                sp.dma_start(x_sb[:, bass.ds(b, 1), :].rearrange("p a t -> p (a t)"),
                             x[bass.ds(b, 1), :, :].rearrange("a p t -> p (a t)")).then_inc(x_in[st.slot(d)], 16)

            def load_cond(st, d):
                b, = ready(st, st.at(d))
                sp.dma_start(cond_all[:, bass.ds(b, 1), :].rearrange("p a t -> p (a t)"),
                             cond[bass.ds(b, 1), :].to_broadcast([P, T])).then_inc(cond_all_in[st.slot(d)], 16)

            def load_batch(st, d):
                load_x(st, d)
                load_cond(st, d)

            s0 = Step(0, 0, RING, B, True)
            load_batch(s0, 0)
            sp.dma_start(cond_sb[:, :], cond).then_inc(cond_in, 16)
            load_batch(s0, 1)
            sp.wait_ge(bias_made, 2)
            for side in range(2):
                sp.dma_start(mask_dram[:, side, :, :],
                             mask2[:, side:side + 1, :].to_broadcast([B, NH, T])).then_inc(mask_out, 16)
            load_batch(s0, 2)

            def write_parts(st, d):
                k = st.slot(d)
                sp.wait_ge(parts_made, st.at(d, 4, 4))
                sp.dma_start(parts_dram[k].rearrange("s p r t -> r (s p) t"),
                             parts[:, k, :, :, :].rearrange("r s p t -> r (s p) t")).then_inc(parts_out[k], 16)

            def read_mask(st, d):
                k = st.slot(d)
                b, = ready(st, st.at(d))
                if not st.first(d, RING):
                    sp.wait_ge(s2_done, st.at(d - RING, NH, NH))
                sp.dma_start(stack[k][ROW_MASK:ROW_MASK + 1, :, :, :],
                             mask_dram[bass.ds(b, 1), :, :, :]).then_inc(stack_in[k], 16)

            def read_parts(st, d):
                k = st.slot(d)
                sp.wait_ge(parts_out[k], st.use(d, 16, 16))
                for side, runs in enumerate((LEFT_RUNS, RIGHT_RUNS)):
                    for row, p, n in runs:
                        src = parts_dram[k][side, p:p + max(n, 1)].rearrange("p (k h) t -> p k (h t)", h=NH)
                        if n > 0:
                            src = src.rearrange("p k w -> (p k) w")
                        else:
                            src = src.to_broadcast([-n, DK, NH * T])
                        sp.dma_start(stack[k][row * DK:(row + abs(n)) * DK, side, :, :].rearrange("r h t -> r (h t)"),
                                     src).then_inc(stack_in[k], 16)

            def write_max(st, d, half):
                sp.wait_ge(neg_copied, st.at(d, 2, half + 1))
                n = NH // 2
                sp.dma_start(stack[st.slot(d)][ROW_MAX:ROW_MAX + 2, 1, half * n:half * n + n, :],
                             neg_rows[:, half, :]).then_inc(max_in[half], 16)

            write_parts(s0, 0)
            sp.wait_ge(mask_out, 32)
            sp.wait_ge(rows_made, 1)
            read_mask(s0, 0)
            read_parts(s0, 0)
            write_parts(s0, 1)
            load_batch(s0, 3)
            sp.dma_start(wo_sb[:, :], woT).then_inc(wo_in, 16)
            sp.dma_start(rt_sb[:, :, :], routerT.rearrange("(k p) e -> p k e", p=P)).then_inc(router_in, 16)

            sp.wait_ge(rows_made, RING)

            def step(st):
                if st.has(1) and not st.first(1, 2):
                    write_parts(st, 1)
                if st.has(-3):
                    t, b, copied = ready(st, st.at(-3, P), st.at(-3), st.at(-3, 1, 1))
                    sp.wait_ge(h_copied, copied)
                    sp.dma_start(rows_dram[bass.ds(t, P), 0:T], h_sb[:, st.slot(-3), :]).then_inc(h_out[st.slot(-3)], 16)
                    sp.dma_start(rows_dram[bass.ds(t, P), T:2 * T],
                                 x_sb[:, bass.ds(b, 1), :].rearrange("p a t -> p (a t)")).then_inc(x_out, 16)
                if st.has(-1):
                    write_max(st, -1, 1)
                if st.has(1):
                    read_mask(st, 1)
                if st.has(4):
                    load_x(st, 4)
                if st.has(1):
                    read_parts(st, 1)
                if st.has(0):
                    write_max(st, 0, 0)
                if st.has(4):
                    load_cond(st, 4)
                if st.peeled and 12 <= st.c < 16:
                    k, e = (st.c - 12) // 2, (st.c - 12) % 2 * (E // 2)
                    sp.dma_start(gu_sb[:, k, e:e + E // 2, :],
                                 guT[e:e + E // 2, k * P:(k + 1) * P, :].rearrange("e p i -> p e i")).then_inc(experts_in, 16)
                if st.peeled and st.c == 16:
                    sp.dma_start(dn_sb[:, :, :], dnT[:, 0:P, :].rearrange("e i t -> i e t")).then_inc(experts_in, 16)
                    sp.dma_start(dn2_sb[:, :, :], dnT[:, P:I, :].rearrange("e i t -> i e t")).then_inc(experts_in, 16)

            attention_steps(sp, step)
            sp.wait_ge(gate_made, 1)
            sp.dma_start(rows_dram[:, 2 * T:ROW].rearrange("(b p) o -> p b o", p=P),
                         gate[:, :].rearrange("p (b o) -> p b o", o=1), allow_slow_non_contiguous=True).then_inc(gate_out, 16)

        @block.tensor
        def _(pe):
            t_ = nc.tensor

            def project_q(st, d):
                pe.wait_ge(x_in[st.slot(d)], st.use(d, 16, 16))
                b = st.at(d)
                if not st.first(d, 1):
                    pe.wait_ge(q_copied, st.at(d))
                t_.matmul(bank[5][:, 0:T], wq_sb[:, :], x_sb[:, bass.ds(b, 1), :].rearrange("p o t -> p (o t)"), start=True, stop=True).then_inc(q_done, 1)

            def turn_values(st, d):
                pe.wait_ge(q_copied, st.at(d, 1, 1))
                if not st.first(d, 2):
                    pe.wait_ge(neg_copied, st.at(d - 2, 2, 2))
                elif not st.first(d, 1):
                    pe.wait_ge(vt_copied, 1)
                for k in range(NT):
                    mm = t_.transpose(bank[6][:, k * P:(k + 1) * P], q_sb[:, st.slot(d), k * P:(k + 1) * P], ident[:, :])
                mm.then_inc(vt_done, 1)

            def turn_max(st, d, half):
                pe.wait_ge(neg_made, st.at(d, 2, half + 1))
                last = d + (2 if half == 1 else 1)
                last = min(st.c + last, B) if st.peeled else st.at(last)
                pe.wait_ge(vt_copied, last if half == 1 else (min(st.c + d + 2, B) if st.peeled else st.at(d, 1, 2)))
                if half == 0 and not st.first(d, 1):
                    pe.wait_ge(neg_copied, st.at(d, 2))
                to = bank[6][:, :].bitcast(BF16)
                for q in range(NT):
                    mm = t_.transpose(to[0:NH, q * P:(q + 1) * P],
                                      neg_max[:, half, q, :, :].rearrange("p a h -> p (a h)"), ident_b[:, :])
                mm.then_inc(neg_turned, 1)

            def scores_for_max(st, h):
                k = st.slot(0)
                if h == 0:
                    pe.wait_ge(stack_in[k], st.use(0, 16 * STACK_DMAS, 16 * STACK_DMAS))
                if h >= 2 or not st.first(0, 1):
                    pe.wait_ge(max_done, st.at(0, NH, h - 1))
                for q in range(NT):
                    mm = t_.matmul(bank[h % 2][:, q * T:(q + 1) * T], stack[k][0:ROWS1, 1, h, q * P:(q + 1) * P],
                                   stack[k][0:ROWS1, 0, h, :], start=True, stop=True)
                mm.then_inc(s1_done, 1)

            def scores_for_exp(st, h):
                k = st.slot(-1)
                if h % 4 == 0:
                    pe.wait_ge(max_in[h // 4], st.at(-1, 16, 16))
                if h >= 2 or not st.first(-1, 1):
                    pe.wait_ge(exp_done, st.at(-1, NH, h - 1))
                for q in range(NT):
                    mm = t_.matmul(bank[2 + h % 2][:, q * T:(q + 1) * T], stack[k][0:ROWS2, 0, h, q * P:(q + 1) * P],
                                   stack[k][0:ROWS2, 1, h, :], start=True, stop=True)
                mm.then_inc(s2_done, 1)

            def apply_probs(st, d, g, k):
                if k == 0:
                    pe.wait_ge(exp_done, st.at(d, NH, HG * (g + 1)))
                if g == 0 and k == 0:
                    if not st.first(d, 1):
                        pe.wait_ge(pv_copied, st.at(d))
                    pe.wait_ge(vt_copied, st.at(d, 1, 1))
                for c in range(HG):
                    mm = t_.matmul(bank[4][c * VC:(c + 1) * VC, g * T:(g + 1) * T], v_sb[:, st.slot(d), k, HG * g + c, :],
                                   probs[:, HG * g + c, k, :], start=(k == 0), stop=(k == NT - 1))
                if k == NT - 1:
                    mm.then_inc(pv_done, 1)

            def turn_products(st):
                pe.wait_ge(pv_copied, st.at(-2, 1, 1))
                if not st.first(-2, 1):
                    pe.wait_ge(lg_copied, st.at(-2))
                for q in range(NT):
                    for g in range(NH // HG):
                        mm = t_.transpose(bank[7][:, (q * NT + g) * P:(q * NT + g + 1) * P],
                                          pv_sb[:, g, q * P:(q + 1) * P], ident[:, :])
                mm.then_inc(pvT_done, 1)

            def turn_context(st):
                pe.wait_ge(norm_done, st.at(-2, 1, 1))
                for k in range(NT):
                    mm = t_.transpose(bank[7][:, k * P:(k + 1) * P], ctx_sb[:, k, :], ident[:, :])
                mm.then_inc(ctxT_done, 1)

            def project_out(st):
                pe.wait_ge(ctxT_copied, st.at(-2, 1, 1))
                if st.first(-2, 1):
                    pe.wait_ge(wo_in, 16)
                t_.matmul(bank[7][:, 0:T], wo_sb[:, :], ctxT[:, :], start=True, stop=True).then_inc(h_done, 1)

            def turn_hidden(st):
                pe.wait_ge(h_copied, st.at(-3, 1, 1))
                for k in range(NT):
                    mm = t_.transpose(bank[7][:, k * P:(k + 1) * P], h_sb[:, st.slot(-3), k * P:(k + 1) * P], ident[:, :])
                mm.then_inc(hT_done, 1)

            def router(st):
                pe.wait_ge(hT_copied, st.at(-3, 1, 1))
                if st.first(-3, 1):
                    pe.wait_ge(router_in, 16)
                for k in range(NT):
                    mm = t_.matmul(bank[7][:, 0:E], hT[:, k, :], rt_sb[:, k, :], start=(k == 0), stop=(k == NT - 1))
                mm.then_inc(lg_done, 1)

            pe.wait_ge(wq_in, 16)
            pe.wait_ge(consts_made, 7)
            s0 = Step(0, 0, RING, B, True)
            project_q(s0, 0)
            project_q(s0, 1)
            turn_values(s0, 0)

            def step(st):
                for h in range(NH):
                    if st.has(0):
                        scores_for_max(st, h)
                    if st.has(-1):
                        scores_for_exp(st, h)
                    if h == 5 and st.has(0):
                        turn_max(st, 0, 0)
                    if h in (0, 1) and st.has(-2):
                        apply_probs(st, -2, 1, h)
                    if h == 0 and st.has(-1):
                        turn_max(st, -1, 1)
                    if h == 0 and st.has(-3):
                        turn_hidden(st)
                    if h == 2 and st.has(2):
                        project_q(st, 2)
                    if h == 1 and st.has(-3):
                        router(st)
                    if h == 3 and st.has(1):
                        turn_values(st, 1)
                    if h == 3 and st.has(-2):
                        turn_products(st)
                    if h == 6 and st.has(-2):
                        turn_context(st)
                    if h in (5, 6) and st.has(-1):
                        apply_probs(st, -1, 0, h - 5)
                    if h == 7 and st.has(-2):
                        project_out(st)

            attention_steps(pe, step)

            pe.wait_ge(added, B)
            t_.matmul(bank[0][:, 0:B * E], before[:, :], onehot[:, :, :].rearrange("p b e -> p (b e)"), start=True, stop=False)
            t_.matmul(bank[0][:, 0:B * E], ones_b[:, :], earlier[:, 0:B, :].rearrange("p b e -> p (b e)"), start=False, stop=True)
            t_.matmul(bank[1][:, 0:E], ones_b[:, :], earlier[:, B, :], start=True, stop=True).then_inc(ranks_done, 1)
            pe.wait_ge(cols_made, 1)
            order = list(range(HOT, B)) + list(range(HOT))
            pe.wait_ge(rest_hot_made, B - HOT)
            for b in order:
                if b < HOT:
                    pe.wait_ge(lo_hot_made, b + 1)
                mm = t_.matmul(bank[2][:, 0:2 * NS], lo_hot[:, b, :], cols[:, b, :, :].rearrange("p a s -> p (a s)"),
                               start=(b == order[0]), stop=(b == order[-1]))
            mm.then_inc(table_done, 1)

            pe.wait_ge(experts_found, 1)
            pe.wait_ge(experts_in, 96)

            def expert_of(st, d):
                m = st.at(d)
                return pe.value_load(expert_i[0:1, bass.ds(m, 1)], min_val=0, max_val=E - 1)

            def slot_step(st):
                if st.has(-1):
                    e_up = expert_of(st, -1)
                if st.has(-3):
                    e_down = expert_of(st, -3)
                if st.has(0):
                    c = st.slot(0)
                    pe.wait_ge(got_in[c], st.use(0, 16, 16))
                    if not st.first(0, 1):
                        pe.wait_ge(g_copied, st.at(0))
                    for k in range(NT):
                        mm = t_.transpose(bank[0][:, k * P:(k + 1) * P], got[c][:, k * P:(k + 1) * P], ident[:, :])
                    mm.then_inc(g_turned, 1)
                if st.has(-1):
                    m2 = (st.c - 1) % 2
                    pe.wait_ge(g_copied, st.at(-1, 1, 1))
                    if not st.first(-1, 2):
                        pe.wait_ge(act_done, st.at(-1, 1, -1))
                    for k in range(NT):
                        mm = t_.matmul(bank[1 + m2][:, 0:I2], gotT[:, m2, k, :],
                                       gu_sb[:, k, bass.ds(e_up, 1), :].rearrange("p a i -> p (a i)"),
                                       start=(k == 0), stop=(k == NT - 1))
                    mm.then_inc(gu_done, 1)
                if st.has(-2):
                    m2 = (st.c - 2) % 2
                    pe.wait_ge(act_done, st.at(-2, 1, 1))
                    if not st.first(-2, 1):
                        pe.wait_ge(a_copied, st.at(-2))
                    t_.transpose(bank[3][:, 0:P], act_sb[:, m2, 0:P], ident[:, :])
                    t_.transpose(bank[3][0:IR, P:2 * P], act_sb[:, m2, P:I], ident[:, :]).then_inc(a_turned, 1)
                if st.has(-3):
                    m2 = (st.c - 3) % 2
                    pe.wait_ge(a_copied, st.at(-3, 1, 1))
                    if not st.first(-3, 2):
                        pe.wait_ge(y_done, st.at(-3, 1, -1))
                    t_.matmul(bank[4 + m2][:, 0:T], actT[:, m2, 0, :],
                              dn_sb[:, bass.ds(e_down, 1), :].rearrange("p a t -> p (a t)"), start=True, stop=False)
                    t_.matmul(bank[4 + m2][:, 0:T], actT[0:IR, m2, 1, :],
                              dn2_sb[:, bass.ds(e_down, 1), :].rearrange("p a t -> p (a t)"),
                              start=False, stop=True).then_inc(dn_done, 1)

            expert_steps(pe, slot_step)

        @block.scalar
        def _(act):
            a = nc.scalar

            def copy_q(st, d):
                pe_b = bank[5][:, 0:T]
                act.wait_ge(q_done, st.at(d, 1, 1))
                if not st.first(d, RING):
                    act.wait_ge(parts_made, st.at(d - RING, 4, 4))
                    act.wait_ge(vt_done, st.at(d - RING, 1, 1))
                    act.wait_ge(parts_out[st.slot(d)], st.use(d, 16))
                a.copy(q_sb[:, st.slot(d), :], pe_b)
                a.copy(parts[:, st.slot(d), 0, 0, :], pe_b).then_inc(q_copied, 1)

            def copy_values(st, d):
                act.wait_ge(vt_done, st.at(d, 1, 1))
                a.copy(v_sb[:, st.slot(d), :, :, 0:DK],
                              bank[6][:, 0:T].rearrange("p (k c h) -> p k h c", k=NT, h=NH)).then_inc(vt_copied, 1)

            def exponential(st, h):
                act.wait_ge(s2_done, st.at(-1, NH, h + 1))
                if h % HG == 0 and not st.first(-1, 1):
                    act.wait_ge(pv_done, st.at(-1, 2, h // HG - 1))
                a.activation(probs[:, h, :, :].rearrange("p k t -> p (k t)"), bank[2 + h % 2][:, 0:NT * T], ACT.Exp,
                             scale=float(DK) ** -0.5).then_inc(exp_done, 1)

            s0 = Step(0, 0, RING, B, True)
            copy_q(s0, 0)
            copy_q(s0, 1)
            act.wait_ge(values_made, 2)
            copy_values(s0, 0)

            def step(st):
                for h in range(NH):
                    if st.has(-1):
                        exponential(st, h)
                    if h == 0 and st.has(-3):
                        act.wait_ge(hT_done, st.at(-3, 1, 1))
                        a.copy(hT[:, :, :].rearrange("p k d -> p (k d)"), bank[7][:, 0:T]).then_inc(hT_copied, 1)
                    if h == 1 and st.has(-2):
                        act.wait_ge(pv_done, st.at(-2, 2, 2))
                        if not st.first(-2, 1):
                            act.wait_ge(pvT_done, st.at(-2))
                        a.copy(pv_sb[:, :, :].rearrange("p g t -> p (g t)"), bank[4][:, :]).then_inc(pv_copied, 1)
                    if h == 2 and st.has(2):
                        copy_q(st, 2)
                    if h == 1 and st.has(-3):
                        act.wait_ge(lg_done, st.at(-3, 1, 1))
                        if not st.first(-3, 1):
                            act.wait_ge(best_made, st.at(-3))
                        a.copy(logits[:, st.slot(-3), :], bank[7][:, 0:E]).then_inc(lg_copied, 1)
                    if h == 3 and st.has(1):
                        copy_values(st, 1)
                    if h == 6 and st.has(-2):
                        act.wait_ge(ctxT_done, st.at(-2, 1, 1))
                        a.copy(ctxT[:, :], bank[7][:, 0:T]).then_inc(ctxT_copied, 1)
                    if h == 7 and st.has(-2):
                        act.wait_ge(h_done, st.at(-2, 1, 1))
                        if not st.first(-2, RING):
                            act.wait_ge(h_out[st.slot(-2)], st.use(-2, 16))
                        a.copy(h_sb[:, st.slot(-2), :], bank[7][:, 0:T]).then_inc(h_copied, 1)

            attention_steps(act, step)
            act.wait_ge(best_made, B)
            a.activation(gate[:, :], gap[:, :], ACT.Exp).then_inc(gap_exp, 1)
            act.wait_ge(gap_exp, 1)
            a.activation(silu[:, 0, 0:B], gap[:, :], ACT.Silu)

            def slot_step(st):
                if st.has(0):
                    act.wait_ge(g_turned, st.at(0, 1, 1))
                    if not st.first(0, 2):
                        act.wait_ge(gu_done, st.at(0, 1, -1))
                    a.copy(gotT[:, st.c % 2, :, :].rearrange("p k s -> p (k s)"), bank[0][:, 0:2 * P]).then_inc(g_copied, 1)
                if st.has(-1):
                    m2 = (st.c - 1) % 2
                    act.wait_ge(gu_done, st.at(-1, 1, 1))
                    if not st.first(-1, 2):
                        act.wait_ge(act_done, st.at(-1, 1, -1))
                    a.activation(silu[:, m2, :], bank[1 + m2][:, 0:I], ACT.Silu).then_inc(silu_done, 1)
                if st.has(-2):
                    m2 = st.c % 2
                    act.wait_ge(a_turned, st.at(-2, 1, 1))
                    if not st.first(-2, 2):
                        act.wait_ge(dn_done, st.at(-2, 1, -1))
                    a.copy(actT[:, m2, 0, :], bank[3][:, 0:P])
                    a.copy(actT[0:IR, m2, 1, :], bank[3][0:IR, P:2 * P]).then_inc(a_copied, 1)

            expert_steps(act, slot_step)

        @block.vector
        def _(dve):
            v = nc.vector
            dve.wait_ge(cond_in, 16)
            v.tensor_scalar(mask2[:, 0, :], cond_sb[:, :], -NEG, NEG, ALU.mult, ALU.add).then_inc(bias_made, 1)
            v.tensor_copy(mask2[:, 1, :], cond_sb[:, :]).then_inc(bias_made, 1)
            ones_pair = float(np.frombuffer(np.array([0x3F803F80], np.uint32).tobytes(), np.float32)[0])

            def ones_rows(k):
                v.memset(stack[k][ROW_MASK:P, 0, :, :].rearrange("p h t -> p (h t)").bitcast(F32), ones_pair).then_inc(rows_made, 1)

            ones_rows(0)
            pt = parts[:, 0]
            dve.wait_ge(q_copied, 1)
            v.tensor_tensor(pt[:, 0, 1, :], q_sb[:, 0, :], pt[:, 0, 0, :], ALU.subtract)
            v.tensor_tensor(first_rest[:, :], q_sb[:, 0, :], pt[:, 0, 0, :], ALU.subtract).then_inc(parts_step, 1)
            dve.wait_ge(parts_step, 1)
            v.tensor_tensor(pt[:, 0, 2, :], first_rest[:, :], pt[:, 0, 1, :], ALU.subtract).then_inc(parts_made, 1)
            dve.wait_ge(parts_made, 1)
            dve.wait_ge(cond_all_in[0], 16)
            for p in range(3):
                v.tensor_tensor(pt[:, 1, p, :], pt[:, 0, p, :], cond_all[:, 0, :], ALU.mult).then_inc(parts_made, 1)
            for k in range(1, RING):
                ones_rows(k)

            def copy_max(st, d, half):
                dve.wait_ge(neg_turned, st.at(d, 2, half + 1))
                if not st.first(d, 1):
                    dve.wait_ge(max_in[half], st.at(d, 16))
                v.tensor_copy(neg_rows[:, half, :], bank[6][:, :].bitcast(BF16)[0:NH, 0:T]).then_inc(neg_copied, 1)

            def negate_max(st, half):
                dve.wait_ge(max_done, st.at(0, NH, 4 * half + 4))
                v.tensor_scalar(neg_max[:, half, :, 0, :], row_max[:, half, :, :], -1.0, None, ALU.mult).then_inc(neg_hi_made, 1)
                dve.wait_ge(neg_hi_made, st.at(0, 2, half + 1))
                v.scalar_tensor_tensor(out=neg_max[:, half, :, 1, :], in0=row_max[:, half, :, :], scalar=-1.0,
                                       in1=neg_max[:, half, :, 0, :], op0=ALU.mult, op1=ALU.subtract).then_inc(neg_made, 1)

            dve.wait_ge(iotas_made, 8)

            def normalize(st):
                dve.wait_ge(pvT_done, st.at(-2, 1, 1))
                pv = bank[7][:, :].rearrange("p (g c) -> p g c", c=VC)
                v.reciprocal(rsum[:, :], pv[:, :, DK]).then_inc(recip_done, 1)
                dve.wait_ge(recip_done, st.at(-2, 1, 1))
                v.tensor_tensor(ctx_sb[:, :, :].rearrange("p k (h c) -> p (k h) c", h=NH), pv[:, :, 0:DK],
                                rsum[:, :].rearrange("p (g o) -> p g o", o=1).to_broadcast([P, NT * NH, DK]),
                                ALU.mult).then_inc(norm_done, 1)

            def step(st):
                for h in range(NH):
                    if h == 2 and st.has(-3):
                        dve.wait_ge(lg_copied, st.at(-3, 1, 1))
                    if st.has(0):
                        dve.wait_ge(s1_done, st.at(0, NH, h + 1))
                        v.tensor_reduce(row_max[:, h // 4, :, h % 4:h % 4 + 1],
                                        bank[h % 2][:, 0:NT * T].rearrange("p (q k) -> p q k", q=NT), AX.X, ALU.max).then_inc(max_done, 1)
                    if h == 0 and st.has(-1):
                        copy_max(st, -1, 1)
                    if h in (2, 5, 6) and st.has(-3):
                        b, k = st.at(-3), st.slot(-3)
                        if h == 2:
                            v.max(out=top[:, k, :], in_=logits[:, k, :]).then_inc(top_made, 1)
                        elif h == 5:
                            dve.wait_ge(top_made, st.at(-3, 1, 1))
                            v.tensor_tensor(gap[:, bass.ds(b, 1)], top[:, k, 1:2], top[:, k, 0:1], ALU.subtract)
                            v.max_index(out=best[:, k, :], in_max=top[:, k, :], in_values=logits[:, k, :]).then_inc(best_made, 1)
                        else:
                            dve.wait_ge(best_made, st.at(-3, 1, 1))
                            v.tensor_tensor(onehot[:, bass.ds(b, 1), :].rearrange("p a e -> p (a e)"), iota_e[:, :],
                                            best[:, k, 0:1].to_broadcast([P, E]), ALU.is_equal).then_inc(onehot_made, 1)
                    if h == 3 and st.has(0):
                        negate_max(st, 0)
                    if h == 3 and st.has(-2):
                        normalize(st)
                    if h == 4 and st.has(0):
                        copy_max(st, 0, 0)
                if st.has(0):
                    negate_max(st, 1)

            attention_steps(dve, step)

            marked = [0]

            def mark(ins):
                marked[0] += 1
                ins.then_inc(route_step, 1)
                return marked[0]

            def need(step):
                dve.wait_ge(route_step, step)

            def per_token(ap, n):
                return ap.rearrange("p (b o) -> p b o", o=1).to_broadcast([P, B, n])

            dve.wait_ge(gap_exp, 1)
            need(mark(v.tensor_scalar(gate[:, :], gate[:, :], 1.0, None, ALU.add)))
            v.reciprocal(gate[:, :], gate[:, :]).then_inc(gate_made, 1)

            dve.wait_ge(ranks_done, 1)
            is_filled = mark(v.tensor_tensor(filled[:, :, :], bank[1][:, 0:E].rearrange("p (e o) -> p e o", o=1).to_broadcast([P, E, B]),
                                             fill[:, :, :], ALU.is_gt))
            is_rank_of = mark(v.tensor_tensor(rank_of[:, :, :], bank[0][:, 0:B * E].rearrange("p (b e) -> p b e", b=B),
                                              onehot[:, :, :], ALU.mult))
            need(is_filled)
            is_tiles = mark(v.tensor_reduce(tiles[:, :], filled[:, :, :], AX.X, ALU.add))
            need(is_rank_of)
            is_rank = mark(v.tensor_reduce(rank[:, :], rank_of[:, :, :], AX.X, ALU.add))
            need(is_tiles)
            is_tiles_to = mark(v.tensor_tensor_scan(tiles_to[:, :], one_e[:, :], tiles[:, :], 0.0, ALU.mult, ALU.add))
            need(is_rank)
            is_rank_i = mark(v.tensor_copy(rank_i[:, :], rank[:, :]))
            need(is_tiles_to)
            is_start = mark(v.tensor_tensor(start[:, :], tiles_to[:, :], tiles[:, :], ALU.subtract))
            need(is_rank_i)
            is_lo_i = mark(v.tensor_scalar(lo_i[:, :], rank_i[:, :], P - 1, None, ALU.bitwise_and))
            is_hi_i = mark(v.tensor_scalar(hi_i[:, :], rank_i[:, :], 7, None, ALU.logical_shift_right))
            need(is_start)
            is_start_of = mark(v.tensor_tensor(start_of[:, :, :], start[:, :].rearrange("p (o e) -> p o e", o=1).to_broadcast([P, B, E]),
                                               onehot[:, :, :], ALU.mult))
            need(is_lo_i)
            v.tensor_copy(lo[:, :], lo_i[:, :]).then_inc(lo_made, 1)
            need(is_hi_i)
            mark(v.tensor_copy(rank_hi[:, :], hi_i[:, :]))
            need(is_start_of)
            is_first = mark(v.tensor_reduce(first_tile[:, :], start_of[:, :, :], AX.X, ALU.add))
            need(is_first)
            is_hi = mark(v.tensor_tensor(hi[:, :], first_tile[:, :], rank_hi[:, :], ALU.add))
            need(is_hi)
            is_hot = mark(v.tensor_tensor(hi_hot[:, :, :], iota_s[:, :, :], per_token(hi[:, :], NS), ALU.is_equal))
            dve.wait_ge(lo_made, 1)
            for b in range(HOT):
                v.tensor_scalar(lo_hot[:, b, :], iota_col[:, :], lo[:, b:b + 1], None, ALU.is_equal).then_inc(lo_hot_made, 1)
                if b == 0:
                    need(is_hot)
                    v.tensor_tensor(cols[:, :, 0, :], hi_hot[:, :, :], iota_b[:, :, :], ALU.mult)
                    v.tensor_tensor(cols[:, :, 1, :], hi_hot[:, :, :], iota_p[:, :, :], ALU.mult).then_inc(cols_made, 1)
            to_b = tiles_to[0:1, :].rearrange("p (o e) -> p o e", o=1).to_broadcast([1, NS, E])
            is_cmp = mark(v.tensor_tensor(expert_cmp[:, :, :], tile_e[:, :, :], to_b, ALU.is_ge))
            need(is_cmp)
            is_expert = mark(v.tensor_reduce(expert_f[:, :], expert_cmp[:, :, :], AX.X, ALU.add))
            need(is_expert)
            v.tensor_scalar(expert_i[:, :], expert_f[:, :], float(E - 1), None, ALU.min).then_inc(experts_found, 1)
            dve.wait_ge(table_done, 1)
            need(mark(v.tensor_scalar(table[:, :], bank[2][:, 0:NS], float(P), -float(P), ALU.mult, ALU.add)))
            need(mark(v.tensor_tensor(token[:, :], table[:, :], bank[2][:, NS:2 * NS], ALU.add)))
            v.tensor_scalar(take_i[:, :], token[:, :], 0.0, None, ALU.max).then_inc(take_made, 1)
            need(mark(v.tensor_scalar(empty[:, :], token[:, :], 0.0, float(2 * TOK), ALU.is_lt, ALU.mult)))
            v.tensor_tensor(put_i[:, :], token[:, :], empty[:, :], ALU.add).then_inc(put_made, 1)

            def slot_step(st):
                if st.has(-1):
                    m2 = (st.c - 1) % 2
                    dve.wait_ge(silu_done, st.at(-1, 1, 1))
                    if not st.first(-1, 2):
                        dve.wait_ge(a_turned, st.at(-1, 1, -1))
                    dve.wait_ge(got_in[st.slot(-1)], st.use(-1, 16, 16))
                    v.scalar_tensor_tensor(out=act_sb[:, m2, :], in0=silu[:, m2, :], scalar=got[st.slot(-1)][:, 2 * T:ROW],
                                           in1=bank[1 + m2][:, I:I2], op0=ALU.mult, op1=ALU.mult).then_inc(act_done, 1)
                if st.has(-3):
                    m2, c = (st.c - 3) % 2, st.slot(-3)
                    dve.wait_ge(dn_done, st.at(-3, 1, 1))
                    if not st.first(-3, SRING):
                        dve.wait_ge(y_out[c], st.use(-3, 16))
                    v.tensor_tensor(y_sb[c][:, :], bank[4 + m2][:, 0:T], got[c][:, T:2 * T], ALU.add).then_inc(y_done, 1)

            expert_steps(dve, slot_step)


def kernel(x, cond_2048, L0_cond_Wq, L0_cond_Wo, L0_ffn_router_w, L0_ffn_gate_w, L0_ffn_up_w, L0_ffn_down_w):
    import numpy as np
    import concourse.bacc as bacc
    from concourse import mybir as mb
    from concourse.bass_utils import run_bass_kernel_spmd as run

    dk = L0_cond_Wq.shape[0] // NH
    wqT = np.asarray(L0_cond_Wq).reshape(NH, dk, -1).transpose(2, 1, 0).reshape(-1, NH * dk)
    data = {
        "x": x, "cond": cond_2048, "wqT": wqT, "woT": L0_cond_Wo.T, "routerT": L0_ffn_router_w.T,
        "guT": np.concatenate([L0_ffn_gate_w.transpose(0, 2, 1), L0_ffn_up_w.transpose(0, 2, 1)], axis=2),
        "dnT": L0_ffn_down_w.transpose(0, 2, 1),
    }
    nc = bacc.Bacc("TRN2", target_bir_lowering=False, num_devices=1)
    arrays, args = {}, []
    for name, a in data.items():
        a = np.ascontiguousarray(a)
        arrays[f"in_{name}"] = a
        args.append(nc.dram_tensor(f"in_{name}", a.shape, mb.dt.from_np(a.dtype), kind="ExternalInput").ap())
    args.append(nc.dram_tensor("out_0", x.shape, mb.dt.from_np(x.dtype), kind="ExternalOutput").ap())
    adaln_ffn(nc, *args)
    r = run(nc, [arrays], core_ids=[0])
    return r.results[0]["out_0"]
```
